# Optimizing a Trainium2 kernel written in Bass

```python
import numpy as np
import jax
import jax.numpy as jnp

def _softmax(x, axis=-1):
    return jax.nn.softmax(x, axis=axis)

def _gelu(x):
    return jax.nn.gelu(x, approximate=True)

def _silu(x):
    return jax.nn.silu(x)

def _sigmoid(x):
    return jax.nn.sigmoid(x)

def _layernorm(x, axis=-1, eps=1e-05):
    m = jnp.mean(x, axis=axis, keepdims=True)
    v = jnp.var(x, axis=axis, keepdims=True)
    return (x - m) / jnp.sqrt(v + eps)

def _scatter_add(tgt, idx, src, axis=0):
    return tgt.at[idx].add(src)

def _segment_sum(src, seg, n):
    return jax.ops.segment_sum(src, seg, n)
kernel_name = 'mk_cond_resid_d1_seqx_r4_8c6c49'

def setup_inputs(seed: int=0):
    np.random.seed(seed)
    _w = jnp.asarray

    def _rec_inputs():
        import jax
        import jax.numpy as jnp
        _rk = jax.random.key(seed)
        x = -0.0002928 + 1 * jax.random.normal(jax.random.fold_in(_rk, 1), (64, 64, 256), jnp.float32)
        _lenS = 64 - jax.random.randint(jax.random.fold_in(_rk, 7), (64,), 0, max(1, 64 // 4) + 1, jnp.int32)
        _lenS2 = 64 - jax.random.randint(jax.random.fold_in(_rk, 8), (64,), 0, max(1, 64 // 4) + 1, jnp.int32)
        cond_256 = -0.106481 + 1.03144 * jax.random.normal(jax.random.fold_in(_rk, 11), (64, 64), jnp.float32)
        return (x, cond_256)
    x, cond_256 = _rec_inputs()

    def _L0_cond_setup():
        import jax, jax.numpy as jnp
        import numpy as np
        TOP_K = 2
        EPS = 1e-06
        B, S, H, G, E, M = (2, 512, 256, 64, 8, 512)
        key = jax.random.key(seed)
        ks = jax.random.split(key, 16)
        s_h = 1.0 / np.sqrt(H)
        s_g = 1.0 / np.sqrt(G)
        s_m = 1.0 / np.sqrt(M)
        return {'x': jax.random.normal(ks[0], (B, S, H), jnp.float32), 'genre_embed': jax.random.normal(ks[1], (B, 1, G), jnp.float32), 'rms_w': jnp.ones((H,), jnp.float32), 'wg_W': jax.random.normal(ks[2], (H, E), jnp.float32) * s_h, 'wg_b': jnp.zeros((E,), jnp.float32), 'gg_W': jax.random.normal(ks[3], (G, E), jnp.float32) * s_g, 'gg_b': jnp.zeros((E,), jnp.float32), 'W1': jax.random.normal(ks[4], (E, H, M), jnp.float32) * s_h, 'b1': jnp.zeros((E, M), jnp.float32), 'W2': jax.random.normal(ks[5], (E, M, M), jnp.float32) * s_m, 'b2': jnp.zeros((E, M), jnp.float32), 'W3': jax.random.normal(ks[6], (E, M, H), jnp.float32) * s_m, 'b3': jnp.zeros((E, H), jnp.float32)}
    _L0_cond_all = _L0_cond_setup()
    _L0_cond_in = {k: v for k, v in _L0_cond_all.items() if k in ('rms_w', 'wg_W', 'wg_b', 'gg_W', 'gg_b', 'W1', 'b1', 'W2', 'b2', 'W3', 'b3')}
    del _L0_cond_all
    return {'x': x, 'cond_256': cond_256, 'L0_cond_rms_w': _L0_cond_in['rms_w'], 'L0_cond_wg_W': _L0_cond_in['wg_W'], 'L0_cond_wg_b': _L0_cond_in['wg_b'], 'L0_cond_gg_W': _L0_cond_in['gg_W'], 'L0_cond_gg_b': _L0_cond_in['gg_b'], 'L0_cond_W1': _L0_cond_in['W1'], 'L0_cond_b1': _L0_cond_in['b1'], 'L0_cond_W2': _L0_cond_in['W2'], 'L0_cond_b2': _L0_cond_in['b2'], 'L0_cond_W3': _L0_cond_in['W3'], 'L0_cond_b3': _L0_cond_in['b3']}

def reference(x, cond_256, L0_cond_rms_w, L0_cond_wg_W, L0_cond_wg_b, L0_cond_gg_W, L0_cond_gg_b, L0_cond_W1, L0_cond_b1, L0_cond_W2, L0_cond_b2, L0_cond_W3, L0_cond_b3):
    import jax
    import jax.numpy as jnp

    def _L0_cond_ref(x, genre_embed, rms_w, wg_W, wg_b, gg_W, gg_b, W1, b1, W2, b2, W3, b3):
        import jax, jax.numpy as jnp
        import numpy as np
        TOP_K = 2
        EPS = 1e-06
        E = W1.shape[0]
        var = jnp.mean(x * x, axis=-1, keepdims=True)
        xn = rms_w * (x * jax.lax.rsqrt(var + EPS))
        gate = xn @ wg_W + wg_b + (genre_embed @ gg_W + gg_b)
        gate_w = jax.nn.softmax(gate, axis=-1)
        topk_w, topk_i = jax.lax.top_k(gate_w, TOP_K)
        cw = jnp.sum(jax.nn.one_hot(topk_i, E, dtype=x.dtype) * topk_w[..., None], axis=-2)
        h1 = jax.nn.relu(jnp.einsum('bsh,ehm->bsem', x, W1) + b1)
        h2 = jax.nn.relu(jnp.einsum('bsem,emn->bsen', h1, W2) + b2)
        out_e = jnp.einsum('bsen,enh->bseh', h2, W3) + b3
        return jnp.einsum('bseh,bse->bsh', out_e, cw)
    x = x + _L0_cond_ref(x, cond_256[:, None, :], L0_cond_rms_w, L0_cond_wg_W, L0_cond_wg_b, L0_cond_gg_W, L0_cond_gg_b, L0_cond_W1, L0_cond_b1, L0_cond_W2, L0_cond_b2, L0_cond_W3, L0_cond_b3)
    return x

_drawn_inputs = setup_inputs


def setup_inputs(seed=0):
    import zlib

    import numpy as np

    out = dict(_drawn_inputs(seed))
    spreads = {'L0_cond_rms_w': (1.0, 0.2),
     'L0_cond_wg_b': (0.0, 0.1),
     'L0_cond_gg_b': (0.0, 0.1),
     'L0_cond_b1': (0.0, 0.32),
     'L0_cond_b2': (0.0, 0.1),
     'L0_cond_b3': (0.0, 0.1)}
    factors = {}
    for name, (base, spread) in spreads.items():
        noise = np.random.default_rng([zlib.crc32(name.encode()), seed]).standard_normal(out[name].shape)
        drawn = base * np.exp(spread * noise) if base else spread * noise
        out[name] = jnp.asarray(drawn.astype(out[name].dtype))
    for name, factor in factors.items():
        out[name] = (out[name] * factor).astype(out[name].dtype)
    return out
```

```python
from contextlib import ExitStack

import concourse.bass as bass
from concourse import mybir

ALU = mybir.AluOpType
ACT = mybir.ActivationFunctionType
AX = mybir.AxisListType
RED = bass.bass_isa.ReduceOp
F32 = mybir.dt.float32
F16 = mybir.dt.float16
I32 = mybir.dt.int32
U32 = mybir.dt.uint32

P = 128
E = 8
H = 256
M = 512
N = 4096
J = N // P
G = 64
KH = H // P
KM = M // P
T = 256
SUB = T // P
TILES = (2 * N - E) // T + E
COLS = TILES * SUB
MAXT = N // T
RING = 3
GROUPS = TILES // RING
assert TILES % RING == 0
CHUNK = 2048
CHUNKS = 2 * E
WE = 2 * CHUNK
W1_AT, W3_AT, W2_AT = 0, KH * M, KH * M + KM * H
STAGES = 3
PRM = 12 + H
TOP = float(2.0 ** 15)
WSCALE = float(2.0 ** 14)
EXPONENT = 0x7F800000
EPS = 1e-6
FAR = 1 << 20
RR = 8
HALF = CHUNK // 2
EXP_AFTER = 3
WEIGHTS_AT = {15: 4, 31: 5, 47: 6, 63: 7}


def build_moe(nc, x, condT, rms_w, wg, gate_b, gg_W, weights, b1, b2, b3, out):
    with ExitStack() as ctx:
        def sb(name, shape, dt):
            return ctx.enter_context(nc.sbuf_tensor(name, shape, dt))

        def sem(name):
            return ctx.enter_context(nc.semaphore(name))

        w_hi = sb("w_hi", [P, E * WE], F16)
        w_lo = sb("w_lo", [P, E * WE], F16)
        stage = sb("stage", [P, STAGES, CHUNK], F32)
        prm = sb("prm", [P, E, PRM], F32)
        area = sb("area", [P, J * H], F32)
        ident = sb("ident", [P, P], F32)
        slots_tab = sb("slots_tab", [P, COLS, 3], I32)
        etile = sb("etile", [P, TILES], I32)
        cur = sb("cur", [P, RING, SUB * 3], I32)
        cprm = sb("cprm", [P, RING, PRM], F32)
        before = sb("before", [P, P], F16)
        ones16 = sb("ones16", [P, P], F16)
        iota_r = sb("iota_r", [P, P], F16)
        iota_c = sb("iota_c", [P, COLS], F16)
        shared = sb("shared", [P, 1536], F32)
        rmsw = sb("rmsw", [P, KH], F32)
        wgs = sb("wgs", [P, KH, E], F32)
        cond_s = sb("cond_s", [G + 2, P], F32)
        ggw_s = sb("ggw_s", [G + 2, E], F32)
        ssq = sb("ssq", [P, J], F32)
        wsq = sb("wsq", [P, CHUNKS, 2], F32)
        fsq = sb("fsq", [P, CHUNKS, 2], F32)
        fpow = sb("fpow", [P, CHUNKS, 2], F32)
        sw = sb("sw", [P, CHUNKS, 2], F32)
        halves = sb("halves", [P, J], F32)
        rank = sb("rank", [P, E], F32)
        small = sb("small", [P, 12, 16], F32)
        tokv = sb("tokv", [P, J], F32)
        k_tile = sb("k_tile", [P, MAXT], F32)
        i_tile = sb("i_tile", [P, TILES], F32)
        sx = small[:, 8, 0:1]

        at = [0]

        def take(cols):
            at[0] += cols
            return area[:, at[0] - cols:at[0]]

        h1_32, h2_32 = take(KM * T), take(KM * T)
        h1_hi, h1_lo, h2_hi, h2_lo = (take(KM * T // 2).bitcast(F16) for _ in range(4))
        xg = take(RING * SUB * H).rearrange("p (s u h) -> p s u h", s=RING, u=SUB)
        xt_hi, xt_lo = (take(KH * T // 2).bitcast(F16) for _ in range(2))
        y32 = take(SUB * H)
        yb = take(RING * SUB * H).rearrange("p (s u h) -> p s u h", s=RING, u=SUB)
        assert at[0] == J * H
        x_sb = area[:, :].rearrange("p (j h) -> p j h", j=J)

        at[0] = 0
        gate, cand, oh1, oh2, total, upto, restart = (take(E * J) for _ in range(7))
        second = take(E * J)
        ex = take(E * J + J)
        sel16 = take(E * J // 2).bitcast(F16)
        cmp_n = take(E * MAXT)
        cmp_t = take(TILES * E)
        et_f = take(TILES)
        cand_ex = take(E * J + J)
        var, rstd, tmp, m1, m2, r1, rs = (take(J) for _ in range(7))
        genre = take(E)
        slot_f = take(2 * J)
        slot_i = take(2 * J).bitcast(I32)
        part_i = take(2 * J).bitcast(I32)
        col_f, row_f = take(2 * J), take(2 * J)
        wt = take(2 * J)
        wt16 = take(J).bitcast(F16)
        wt_h, wt_l = take(2 * J), take(2 * J)
        code, pad, pos_f = take(COLS), take(COLS), take(COLS)
        wsum = take(COLS)
        assert at[0] <= J * H

        def chunk_scale(q, a):
            return sw[:, q, 0:1] if q % 2 else sw[:, q, a:a + 1]

        def unread(first, n):
            return w_lo[:, first:first + n].bitcast(mybir.dt.bfloat16)

        def ej(ap):
            return ap.rearrange("p (e j) -> p e j", e=E)

        def je(ap):
            return ap.rearrange("p (e j) -> p j e", e=E)

        def over_j(ap):
            return ap.unsqueeze(2).to_broadcast([P, E, J])

        def over_e(ap):
            return ap.unsqueeze(1).to_broadcast([P, E, J])

        xT = shared[:, :].rearrange("p (r c) -> p r c", r=3)
        hot_r = shared[:, 0:RR * P // 2].bitcast(F16).rearrange("p (r c) -> p r c", r=RR)
        q_at = RR * P // 2
        hot_q = shared[:, q_at:q_at + RR * 3 * COLS // 2].bitcast(F16)\
            .rearrange("p (r v c) -> p r v c", r=RR, v=3)
        assert q_at + RR * 3 * COLS // 2 <= 1536

        bank = [ctx.enter_context(nc.psum_tensor(f"bank{b}", [P, 512], F32)) for b in range(6)]
        ps_gate, ps_genre = bank[5][:, 0:E * J], bank[5][:, E * J:E * J + E]
        ps_before, ps_total = bank[4][:, 0:E * J], bank[4][:, E * J:2 * E * J]
        ps_slots = bank[3][:, 0:3 * COLS]
        ps_h = [[bank[0], bank[1]], [bank[2], bank[3]]]
        ps_x, ps_y = bank[4], bank[5]

        s_const = sem("s_const")
        s_cid = sem("s_cid")
        s_ones = sem("s_ones")
        s_small = sem("s_small")
        s_x = [sem(f"s_x{c}") for c in range(4)]
        s_w = [sem(f"s_w{c}") for c in range(STAGES)]
        s_out0 = sem("s_out0")
        s_b3 = sem("s_b3")
        s_wgs = sem("s_wgs")
        s_xtp = sem("s_xtp")
        s_xts = sem("s_xts")
        s_gate = sem("s_gate")
        s_ssq = sem("s_ssq")
        s_var = sem("s_var")
        s_pow = sem("s_pow")
        s_wsq = sem("s_wsq")
        s_pool = sem("s_pool")
        s_wpow = sem("s_wpow")
        s_wsc = sem("s_wsc")
        s_whi = sem("s_whi")
        s_wlo = sem("s_wlo")
        s_dve = sem("s_dve")
        s_diff = sem("s_diff")
        s_exp = sem("s_exp")
        s_sel = sem("s_sel")
        s_cnt = sem("s_cnt")
        s_rows = sem("s_rows")
        s_hotr = sem("s_hotr")
        s_hotq = sem("s_hotq")
        s_inv = sem("s_inv")
        s_norm = sem("s_norm")
        s_normp = sem("s_normp")
        s_bnd = sem("s_bnd")
        s_bndp = sem("s_bndp")
        s_tab = sem("s_tab")
        s_ready = sem("s_ready")
        s_own = sem("s_own")
        s_cur = sem("s_cur")
        s_xg = [sem(f"s_xg{s}") for s in range(RING)]
        s_xp = sem("s_xp")
        s_xhi = sem("s_xhi")
        s_xs = sem("s_xs")
        s_l1 = sem("s_l1")
        s_h1f = sem("s_h1f")
        s_h1h = sem("s_h1h")
        s_h1 = sem("s_h1")
        s_l2 = sem("s_l2")
        s_h2f = sem("s_h2f")
        s_h2h = sem("s_h2h")
        s_h2 = sem("s_h2")
        s_l3 = sem("s_l3")
        s_y32 = sem("s_y32")
        s_y = sem("s_y")
        s_add = sem("s_add")

        block = ctx.enter_context(nc.Block())

        @block.sync
        def _(sp):
            for c in range(4):
                js = J // 4
                sp.dma_start(area[:, c * js * H:(c + 1) * js * H],
                             x.rearrange("(p j) h -> p (j h)", p=P)[:, c * js * H:(c + 1) * js * H])\
                  .then_inc(s_x[c], 16)
            for q in range(CHUNKS):
                if q >= STAGES:
                    sp.wait_ge(s_wlo, 2 * (q - STAGES + 1))
                sp.dma_start(stage[:, q % STAGES, :], weights[q]).then_inc(s_w[q % STAGES], 16)
            sp.dma_start(out, x).then_inc(s_out0, 16)

        @block.gpsimd
        def _(pool):
            chain = [0]

            def link(ins):
                chain[0] += 1
                ins.then_inc(s_pool, 1)
                pool.wait_ge(s_pool, chain[0])

            link(pool.memset(ident[:, :], 0.0))
            pool.affine_select(out=ident[:, :], in_=ident[:, :], compare_op=ALU.not_equal, fill=1.0,
                               base=0, pattern=[[-1, P]], channel_multiplier=1).then_inc(s_cid, 1)
            link(pool.memset(halves[:, :], -0.5))
            pool.memset(ones16[:, :], 1.0).then_inc(s_const, 1)
            link(pool.memset(before[:, :], 1.0))
            pool.affine_select(out=before[:, :], in_=before[:, :], compare_op=ALU.is_gt, fill=0.0,
                               base=0, pattern=[[1, P]], channel_multiplier=-1).then_inc(s_const, 1)
            pool.iota(iota_r[:, :], pattern=[[1, P]], base=0, channel_multiplier=0,
                      allow_small_or_imprecise_dtypes=True).then_inc(s_const, 1)
            pool.iota(iota_c[:, :], pattern=[[1, COLS]], base=0, channel_multiplier=0,
                      allow_small_or_imprecise_dtypes=True).then_inc(s_const, 1)
            pool.iota(rank[:, :], pattern=[[-1, E]], base=E, channel_multiplier=0,
                      allow_small_or_imprecise_dtypes=True).then_inc(s_const, 1)

            def weight_norms(q):
                pool.wait_ge(s_wsq, 2 * q + 2)
                w = 2
                if q % 2:
                    link(pool.tensor_tensor(wsq[:, q, 0:1], wsq[:, q, 0:1], wsq[:, q, 1:2], ALU.add))
                    w = 1
                link(pool.partition_all_reduce(fsq[:, q, 0:w], wsq[:, q, 0:w], P, RED.add))
                link(pool.tensor_scalar(fpow[:, q, 0:w], fsq[:, q, 0:w], 1e-30, TOP ** -2, ALU.max, ALU.mult))
                pool.tensor_tensor(fpow[:, q, 0:w], fpow[:, q, 0:w], halves[:, 0:w], ALU.pow)\
                    .then_inc(s_wpow, 1)

            pool.iota(tokv[:, :], pattern=[[1, J]], base=-N // 2, channel_multiplier=J,
                      allow_small_or_imprecise_dtypes=True).then_inc(s_const, 1)
            pool.iota(k_tile[:, :], pattern=[[T, MAXT]], base=0, channel_multiplier=0,
                      allow_small_or_imprecise_dtypes=True).then_inc(s_const, 1)
            pool.iota(i_tile[:, :], pattern=[[1, TILES]], base=0, channel_multiplier=0,
                      allow_small_or_imprecise_dtypes=True).then_inc(s_const, 1)

            pool.wait_ge(s_var, 1)
            pool.tensor_tensor(rstd, var, halves[:, :], ALU.pow).then_inc(s_pow, 1)
            for q in range(4):
                weight_norms(q)
            pool.wait_ge(s_rows, 1)
            for n in range(2 * J):
                if n >= RR:
                    pool.wait_ge(s_inv, n - RR + 1)
                pool.tensor_scalar(hot_r[:, n % RR, :], iota_r[:, :], row_f[:, n:n + 1], None,
                                   ALU.is_equal).then_inc(s_hotr, 1)
                if n + 4 in WEIGHTS_AT:
                    weight_norms(WEIGHTS_AT[n + 4])
            for q in range(8, CHUNKS):
                weight_norms(q)
            nb, rx = small[:, 0, :], small[:, 1, 0:1]
            pool.wait_ge(s_norm, 1)
            pool.partition_all_reduce(small[:, 2, :], nb, P, RED.add).then_inc(s_normp, 1)
            pool.partition_all_reduce(small[:, 3, 0:1], rx, P, RED.max).then_inc(s_normp, 1)
            pool.wait_ge(s_bnd, 1)
            pool.tensor_tensor(small[:, 5, :], small[:, 4, :], halves[:, 0:16], ALU.pow).then_inc(s_bndp, 1)
            pool.tensor_tensor(small[:, 6, 0:1], small[:, 6, 0:1], halves[:, 0:1], ALU.pow).then_inc(s_bndp, 1)

            pool.wait_ge(s_ready, 1)

            def fetch(i, group, s):
                e = pool.value_load(etile[0:1, bass.ds(i, 1)], min_val=0, max_val=E - 1)
                pool.tensor_copy(cur[:, s, :], slots_tab[:, :, :].rearrange("p c v -> p (c v)")
                                 [:, bass.ds(i * (SUB * 3), SUB * 3)]).then_inc(s_cur, 1)
                pool.tensor_copy(cprm[:, s, :], prm[:, :, :].rearrange("p e c -> p (e c)")
                                 [:, bass.ds(e * PRM, PRM)]).then_inc(s_cur, 1)
                pool.wait_ge(s_cur, 2 * i + 2)
                pool.sem_inc(s_own, 1)
                for u in range(SUB):
                    pool.indirect_dma_start(
                        out=xg[:, s, u, :], out_offset=None, in_=x,
                        in_offset=bass.IndirectOffsetOnAxis(ap=cur[:, s, 3 * u:3 * u + 1].bitcast(U32), axis=0),
                    ).then_inc(s_xg[s], 16)

            def add_rows(i, s):
                pool.wait_ge(s_y, 2 * i + 3)
                pool.sem_inc(s_own, 1)
                for u in range(SUB):
                    pool.indirect_dma_start(
                        out=out,
                        out_offset=bass.IndirectOffsetOnAxis(ap=cur[:, s, 3 * u + 1:3 * u + 2].bitcast(U32), axis=0),
                        in_=yb[:, s, u, :], in_offset=None, bounds_check=N - 1, oob_is_err=False,
                        compute_op=ALU.add,
                    ).then_inc(s_add, 16)

            fetch(0, 0, 0)
            fetch(1, 0, 1)
            pool.wait_ge(s_out0, 16)
            fetch(2, 0, 2)
            add_rows(0, 0)
            with pool.Fori(0, GROUPS - 1, 1) as g:
                for s in range(RING):
                    i = g * RING + s + 1
                    pool.wait_ge(s_add, i * SUB * 16)
                    pool.sem_inc(s_own, 1)
                    fetch(i + 2, None, (s + 3) % RING)
                    add_rows(i, (s + 1) % RING)
            for i in range(TILES - 2, TILES):
                pool.wait_ge(s_add, i * SUB * 16)
                add_rows(i, i % RING)
            pool.wait_ge(s_add, TILES * SUB * 16)

        @block.scalar
        def _(act):
            act.dma_start(rmsw[:, :], rms_w).then_inc(s_small, 16)
            act.dma_start(wgs[:, :, :], wg).then_inc(s_small, 16)
            act.dma_start(cond_s[0:G, :], condT).then_inc(s_small, 16)
            act.dma_start(ggw_s[0:G, :], gg_W).then_inc(s_small, 16)
            act.dma_start(ggw_s[G:G + 2, :], gate_b).then_inc(s_small, 16)
            act.dma_start(prm[:, :, 4:8], b1).then_inc(s_small, 16)
            act.dma_start(prm[:, :, 8:12], b2).then_inc(s_small, 16)
            act.dma_start(prm[:, :, 12:PRM], b3.unsqueeze(0).to_broadcast([P, E, H])).then_inc(s_b3, 16)

            for j in range(J):
                if j % (J // 4) == 0:
                    act.wait_ge(s_x[j // (J // 4)], 16)
                act.activation(unread(E * WE - (J - j) * H, H), x_sb[:, j, :], ACT.Square,
                               accum_out=ssq[:, j:j + 1]).then_inc(s_ssq, 1)

            def squares(q):
                act.wait_ge(s_w[q % STAGES], 16 * (q // STAGES + 1))
                for a in range(2):
                    act.activation(unread(q * CHUNK + a * HALF, HALF), stage[:, q % STAGES, a * HALF:(a + 1) * HALF], ACT.Square,
                                   accum_out=wsq[:, q, a:a + 1]).then_inc(s_wsq, 1)

            def high_parts(q):
                act.wait_ge(s_wsc, q + 1)
                for a in range(2):
                    act.activation(w_hi[:, q * CHUNK + a * HALF:q * CHUNK + (a + 1) * HALF],
                                   stage[:, q % STAGES, a * HALF:(a + 1) * HALF], ACT.Copy,
                                   scale=chunk_scale(q, a)).then_inc(s_whi, 1)

            for q in range(CHUNKS):
                squares(q)
                if q >= 1:
                    high_parts(q - 1)
                if q == EXP_AFTER:
                    act.wait_ge(s_diff, 1)
                    act.activation(ex, cand_ex, ACT.Exp).then_inc(s_exp, 1)
            high_parts(CHUNKS - 1)

            def x_high(i):
                act.wait_ge(s_xp, i + 1)
                act.activation(xt_hi, ps_x[:, :], ACT.Copy, scale=sx).then_inc(s_xhi, 1)

            def activate(i, slot, layer):
                done, signal, to = ((s_l1, s_h1f, h1_32), (s_l2, s_h2f, h2_32))[layer]
                for b in range(2):
                    act.wait_ge(done, 2 * i + b + 1)
                    for a in range(2):
                        m = 2 * b + a
                        act.activation(to[:, m * T:(m + 1) * T], ps_h[layer][b][:, a * T:(a + 1) * T], ACT.Relu,
                                       bias=cprm[:, slot, 4 + 4 * layer + m:5 + 4 * layer + m],
                                       scale=cprm[:, slot, layer:layer + 1]).then_inc(signal, 1)

            def weigh(i, slot):
                act.wait_ge(s_y32, i + 2)
                for u in range(SUB):
                    act.activation(yb[:, slot, u, :], y32[:, u * H:(u + 1) * H], ACT.Copy,
                                   scale=cur[:, slot, 3 * u + 2:3 * u + 3].bitcast(F32)).then_inc(s_y, 1)

            def step(i, s, next1=True, next2=True):
                activate(i, s, 1)
                if next1:
                    activate(i + 1, (s + 1) % RING, 0)
                if next2:
                    x_high(i + 2)
                weigh(i, s)

            act.wait_ge(s_ready, 1)
            act.sem_inc(s_y, 1)
            x_high(0)
            activate(0, 0, 0)
            x_high(1)
            with act.Fori(0, GROUPS - 1, 1) as g:
                for s in range(RING):
                    step(g * RING + s, s)
            for s in range(RING):
                i = TILES - RING + s
                step(i, s, i + 1 < TILES, i + 2 < TILES)

        @block.vector
        def _(dve):
            chain = [0]

            def link(ins):
                chain[0] += 1
                ins.then_inc(s_dve, 1)
                dve.wait_ge(s_dve, chain[0])

            def weight_scales(q):
                dve.wait_ge(s_wpow, q + 1)
                w = 1 if q % 2 else 2
                dve.tensor_scalar(sw[:, q, 0:w].bitcast(I32), fpow[:, q, 0:w].bitcast(I32), EXPONENT, None,
                                  ALU.bitwise_and).then_inc(s_wsc, 1)

            def low_parts(q):
                for a in range(2):
                    dve.wait_ge(s_whi, 2 * q + a + 1)
                    at_w = q * CHUNK + a * HALF
                    dve.scalar_tensor_tensor(
                        w_lo[:, at_w:at_w + HALF], stage[:, q % STAGES, a * HALF:(a + 1) * HALF],
                        chunk_scale(q, a), w_hi[:, at_w:at_w + HALF], ALU.mult, ALU.subtract).then_inc(s_wlo, 1)

            def weight_step(q):
                weight_scales(q)
                if q >= 1:
                    low_parts(q - 1)

            dve.memset(cond_s[G:G + 2, :], 1.0).then_inc(s_ones, 1)
            dve.wait_ge(s_small, 7 * 16)
            for k in range(KH):
                ins = dve.tensor_scalar(wgs[:, k, :], wgs[:, k, :], rmsw[:, k:k + 1], None, ALU.mult)
            ins.then_inc(s_wgs, 1)
            for jj in range(J // 2):
                dve.wait_ge(s_xtp, jj + 1)
                if jj >= 3:
                    dve.wait_ge(s_gate, jj - 2)
                dve.tensor_copy(xT[:, jj % 3, :], bank[jj % 4][:, :]).then_inc(s_xts, 1)

            dve.wait_ge(s_gate, J // 2 + 1)
            dve.wait_ge(s_ssq, J)
            dve.tensor_scalar(var, ssq[:, :], 1.0 / H, EPS, ALU.mult, ALU.add).then_inc(s_var, 1)
            weight_step(0)
            dve.wait_ge(s_pow, 1)
            link(dve.tensor_tensor(tmp, rstd, rstd, ALU.mult))
            link(dve.tensor_tensor(tmp, tmp, var, ALU.mult))
            link(dve.tensor_scalar(tmp, tmp, -0.5, 1.5, ALU.mult, ALU.add))
            link(dve.tensor_tensor(rstd, rstd, tmp, ALU.mult))
            link(dve.tensor_tensor(ej(gate), ps_gate.rearrange("p (j e) -> p e j", e=E), over_e(rstd), ALU.mult))
            link(dve.tensor_copy(genre, ps_genre))
            link(dve.tensor_tensor(ej(gate), ej(gate), over_j(genre), ALU.add))
            dve.wait_ge(s_const, 8)
            link(dve.tensor_scalar(tokv[P // 2:P, :], tokv[P // 2:P, :], 1.0, None, ALU.add))

            def pick(scores, top, onehot, best):
                link(dve.tensor_reduce(top, je(scores), AX.X, ALU.max))
                link(dve.tensor_tensor(ej(cand), ej(scores), over_e(top), ALU.is_equal))
                link(dve.tensor_tensor(ej(cand), ej(cand), over_j(rank[:, :]), ALU.mult))
                link(dve.tensor_reduce(best, je(cand), AX.X, ALU.max))
                link(dve.tensor_tensor(ej(onehot), ej(cand), over_e(best), ALU.is_equal))

            pick(gate, m1, oh1, r1)
            weight_step(1)
            link(dve.scalar_tensor_tensor(second, oh1, -3e38, gate, ALU.mult, ALU.add))
            pick(second, m2, oh2, r1)
            dve.tensor_tensor(cand_ex[:, 0:E * J].rearrange("p (e j) -> p e j", e=E), ej(gate), over_e(m1),
                              ALU.subtract)
            dve.tensor_tensor(cand_ex[:, E * J:], m2, m1, ALU.subtract).then_inc(s_diff, 1)
            dve.tensor_tensor(sel16, oh1, oh2, ALU.add).then_inc(s_sel, 1)
            weight_step(2)
            link(dve.memset(restart, 1.0))
            link(dve.memset(ej(restart)[:, :, 0:1], 0.0))
            dve.wait_ge(s_cnt, 1)
            link(dve.tensor_copy(total, ps_total))
            link(dve.tensor_tensor_scan(upto, restart, total, 0.0, ALU.mult, ALU.add))
            count = ej(upto)[:, :, J - 1:J]
            link(dve.tensor_tensor(cmp_n.rearrange("p (e k) -> p e k", e=E), count.to_broadcast([P, E, MAXT]),
                                   k_tile[:, :].unsqueeze(1).to_broadcast([P, E, MAXT]), ALU.is_gt))
            ntile, tend, ones8 = small[:, 9, 0:E], small[:, 10, 0:E], small[:, 11, 0:E]
            link(dve.tensor_reduce(ntile, cmp_n.rearrange("p (e k) -> p e k", e=E), AX.X, ALU.add))
            link(dve.memset(ones8, 1.0))
            link(dve.tensor_tensor_scan(tend, ones8, ntile, 0.0, ALU.mult, ALU.add))
            link(dve.tensor_tensor(cmp_t.rearrange("p (i e) -> p i e", e=E),
                                   i_tile[:, :].unsqueeze(2).to_broadcast([P, TILES, E]),
                                   tend.unsqueeze(1).to_broadcast([P, TILES, E]), ALU.is_ge))
            link(dve.tensor_reduce(et_f, cmp_t.rearrange("p (i e) -> p i e", e=E), AX.X, ALU.add))
            link(dve.tensor_scalar(etile[:, :], et_f, float(E - 1), None, ALU.min))
            link(dve.tensor_tensor(ntile, tend, ntile, ALU.subtract))
            link(dve.tensor_scalar(ntile, ntile, float(T), None, ALU.mult))
            link(dve.tensor_tensor(upto, upto, total, ALU.subtract))
            link(dve.tensor_tensor(upto, upto, ps_before, ALU.add))
            link(dve.tensor_tensor(ej(upto), ej(upto), over_j(ntile), ALU.add))
            for k, oh in enumerate((oh1, oh2)):
                link(dve.tensor_tensor(cand, oh, upto, ALU.mult))
                link(dve.tensor_reduce(slot_f[:, k * J:(k + 1) * J], je(cand), AX.X, ALU.add))
            link(dve.tensor_copy(slot_i, slot_f))
            link(dve.tensor_scalar(part_i, slot_i, P - 1, None, ALU.bitwise_and))
            dve.tensor_copy(row_f, part_i).then_inc(s_rows, 1)
            link(dve.tensor_scalar(slot_i, slot_i, P.bit_length() - 1, None, ALU.logical_shift_right))
            link(dve.tensor_copy(col_f, slot_i))
            weight_step(3)
            dve.wait_ge(s_exp, 1)
            link(dve.tensor_reduce(rs, je(ex[:, 0:E * J]), AX.X, ALU.add))
            link(dve.reciprocal(rs, rs))
            link(dve.tensor_scalar(wt[:, 0:J], rs, WSCALE, None, ALU.mult))
            link(dve.tensor_tensor(wt[:, J:2 * J], ex[:, E * J:], wt[:, 0:J], ALU.mult))
            link(dve.tensor_copy(wt16, wt))
            link(dve.tensor_copy(wt_h, wt16))
            link(dve.tensor_tensor(wt_l, wt, wt_h, ALU.subtract))
            for n in range(2 * J):
                if n >= RR:
                    dve.wait_ge(s_inv, n - RR + 1)
                for v, val in enumerate((tokv[:, n % J:n % J + 1], wt_h[:, n:n + 1], wt_l[:, n:n + 1])):
                    ins = dve.tensor_scalar(hot_q[:, n % RR, v, :], iota_c[:, :], col_f[:, n:n + 1], val,
                                            ALU.is_equal, ALU.mult)
                ins.then_inc(s_hotq, 1)
                if n in WEIGHTS_AT:
                    weight_step(WEIGHTS_AT[n])
            dve.wait_ge(s_inv, 2 * J)
            inv = ps_slots.rearrange("p (v c) -> p v c", v=3)
            link(dve.tensor_copy(code, inv[:, 0, :]))
            link(dve.tensor_scalar(pos_f, code, 0.0, None, ALU.is_gt))
            link(dve.tensor_scalar(pad, code, 0.0, float(FAR), ALU.is_equal, ALU.mult))
            link(dve.scalar_tensor_tensor(code, code, float(N // 2), pos_f, ALU.add, ALU.subtract))
            dve.tensor_copy(slots_tab[:, :, 0], code)
            dve.tensor_tensor(slots_tab[:, :, 1], code, pad, ALU.add)
            link(dve.tensor_copy(wsum, inv[:, 2, :]))
            link(dve.tensor_tensor(wsum, wsum, inv[:, 1, :], ALU.add))
            dve.tensor_scalar(slots_tab[:, :, 2].bitcast(F32), wsum, 1.0 / WSCALE, None, ALU.mult)
            link(dve.tensor_reduce(small[:, 1, 0:1], ssq[:, :], AX.X, ALU.max))
            bias = prm[:, :, 4:12].rearrange("p e (l c) -> p l e c", l=2)
            bsq = cmp_n[:, 0:64].rearrange("p (l e c) -> p l e c", l=2, e=E)
            link(dve.tensor_tensor(bsq, bias, bias, ALU.mult))
            dve.tensor_reduce(small[:, 0, :].rearrange("p (l e) -> p l e", l=2), bsq, AX.X, ALU.add)\
               .then_inc(s_norm, 1)
            for q in range(len(WEIGHTS_AT) + 4, CHUNKS):
                weight_step(q)
            dve.wait_ge(s_normp, 2)
            f1, f2 = fsq[:, 0::2, 0], fsq[:, 1::2, 0]
            b_sq, r2, bnd = small[:, 2, :], small[:, 3, 0:1], small[:, 4, :]
            link(dve.scalar_tensor_tensor(bnd[:, 0:E], f1, r2, b_sq[:, 0:E], ALU.mult, ALU.add))
            link(dve.tensor_scalar(bnd[:, 0:E], bnd[:, 0:E], 2.0, None, ALU.mult))
            link(dve.tensor_tensor(bnd[:, E:], bnd[:, 0:E], f2, ALU.mult))
            link(dve.tensor_tensor(bnd[:, E:], bnd[:, E:], b_sq[:, E:], ALU.add))
            link(dve.tensor_scalar(bnd[:, E:], bnd[:, E:], 2.0, None, ALU.mult))
            link(dve.tensor_scalar(bnd, bnd, 1e-30, TOP ** -2, ALU.max, ALU.mult))
            dve.tensor_scalar(small[:, 6, 0:1], r2, 1e-30, TOP ** -2, ALU.max, ALU.mult).then_inc(s_bnd, 1)
            low_parts(CHUNKS - 1)
            dve.wait_ge(s_bndp, 2)
            sh, ish = small[:, 7, :], small[:, 9, :]
            link(dve.tensor_scalar(sh.bitcast(I32), small[:, 5, :].bitcast(I32), EXPONENT, None, ALU.bitwise_and))
            link(dve.tensor_scalar(sx.bitcast(I32), small[:, 6, 0:1].bitcast(I32), EXPONENT, None, ALU.bitwise_and))
            link(dve.reciprocal(ish, sh))
            link(dve.reciprocal(small[:, 10, 0:1], sx))
            isw, isw3 = small[:, 11, :], small[:, 0, 0:E]
            link(dve.reciprocal(isw, sw[:, :, 0]))
            link(dve.reciprocal(isw3, sw[:, 0::2, 1]))
            link(dve.scalar_tensor_tensor(prm[:, :, 0], sh[:, 0:E], small[:, 10, 0:1], isw[:, 0::2],
                                          ALU.mult, ALU.mult))
            link(dve.tensor_tensor(prm[:, :, 1], ish[:, 0:E], isw[:, 1::2], ALU.mult))
            link(dve.tensor_tensor(prm[:, :, 1], prm[:, :, 1], sh[:, E:], ALU.mult))
            link(dve.tensor_tensor(prm[:, :, 2], ish[:, E:], isw3, ALU.mult))
            link(dve.memset(prm[:, :, 3:4], 0.0))
            for layer in range(2):
                part = prm[:, :, 4 + 4 * layer:8 + 4 * layer]
                link(dve.tensor_tensor(part, part, sh[:, layer * E:(layer + 1) * E].unsqueeze(2)
                                       .to_broadcast([P, E, 4]), ALU.mult))
            dve.wait_ge(s_b3, 16)
            dve.memset(ones8, 1.0).then_inc(s_ready, 1)

            def x_low(i):
                dve.wait_ge(s_xhi, i + 1)
                dve.scalar_tensor_tensor(xt_lo, ps_x[:, :], sx, xt_hi, ALU.mult, ALU.subtract).then_inc(s_xs, 1)

            def split(i, layer):
                full, half_done, signal = ((s_h1f, s_h1h, s_h1), (s_h2f, s_h2h, s_h2))[layer]
                h, hi, lo = ((h1_32, h1_hi, h1_lo), (h2_32, h2_hi, h2_lo))[layer]
                for b in range(2):
                    cols = slice(b * 2 * T, (b + 1) * 2 * T)
                    dve.wait_ge(full, 4 * i + 2 * b + 2)
                    dve.tensor_copy(hi[:, cols], h[:, cols]).then_inc(half_done, 1)
                    dve.wait_ge(half_done, 2 * i + b + 1)
                    dve.tensor_tensor(lo[:, cols], h[:, cols], hi[:, cols], ALU.subtract).then_inc(signal, 1)

            def finish(i, slot):
                dve.wait_ge(s_l3, i + 1)
                dve.wait_ge(s_y, 2 * i + 1)
                dve.scalar_tensor_tensor(
                    y32.rearrange("p (u h) -> p u h", u=SUB), ps_y[:, :].rearrange("p (u h) -> p u h", u=SUB),
                    cprm[:, slot, 2:3], cprm[:, slot, 12:PRM].unsqueeze(1).to_broadcast([P, SUB, H]),
                    ALU.mult, ALU.add).then_inc(s_y32, 1)

            def step(i, s, next1=True, next2=True):
                split(i, 1)
                if next1:
                    split(i + 1, 0)
                if next2:
                    x_low(i + 2)
                finish(i, s)

            dve.sem_inc(s_y32, 1)
            x_low(0)
            split(0, 0)
            x_low(1)
            with dve.Fori(0, GROUPS - 1, 1) as g:
                for s in range(RING):
                    step(g * RING + s, s)
            for s in range(RING):
                i = TILES - RING + s
                step(i, s, i + 1 < TILES, i + 2 < TILES)

        @block.tensor
        def _(pe):
            def transposes(jj):
                if jj % 4 == 0:
                    pe.wait_ge(s_x[jj // 4], 16)
                if jj >= 4:
                    pe.wait_ge(s_xts, jj - 3)
                for k in range(KH):
                    for d in range(2):
                        c = (k * 2 + d) * P
                        ins = nc.tensor.transpose(bank[jj % 4][:, c:c + P],
                                                  x_sb[:, 2 * jj + d, k * P:(k + 1) * P], ident[:, :])
                ins.then_inc(s_xtp, 1)

            def gates(jj):
                pe.wait_ge(s_xts, jj + 1)
                for d in range(2):
                    for k in range(KH):
                        c = (k * 2 + d) * P
                        ins = nc.tensor.matmul(ps_gate[:, (2 * jj + d) * E:(2 * jj + d + 1) * E],
                                               xT[:, jj % 3, c:c + P], wgs[:, k, :],
                                               start=(k == 0), stop=(k == KH - 1))
                ins.then_inc(s_gate, 1)

            pe.wait_ge(s_cid, 1)
            transposes(0)
            pe.wait_ge(s_wgs, 1)
            for jj in range(1, J // 2):
                transposes(jj)
                gates(jj - 1)
            gates(J // 2 - 1)
            pe.wait_ge(s_ones, 1)
            nc.tensor.matmul(ps_genre, cond_s[:, :], ggw_s[:, :], start=True, stop=True).then_inc(s_gate, 1)
            pe.wait_ge(s_const, 8)
            pe.wait_ge(s_sel, 1)
            nc.tensor.matmul(ps_before, before[:, :], sel16, start=True, stop=True)
            nc.tensor.matmul(ps_total, ones16[:, :], sel16, start=True, stop=True).then_inc(s_cnt, 1)
            for n in range(2 * J):
                pe.wait_ge(s_hotr, n + 1)
                pe.wait_ge(s_hotq, n + 1)
                nc.tensor.matmul(ps_slots, hot_r[:, n % RR, :], hot_q[:, n % RR, :, :].rearrange("p v c -> p (v c)"),
                                 start=(n == 0), stop=(n == 2 * J - 1)).then_inc(s_inv, 1)

            def transpose_x(i, slot, turn):
                pe.wait_ge(s_xg[slot], turn * SUB * 16)
                if not (isinstance(i, int) and i == 0):
                    pe.wait_ge(s_xs, i)
                for k in range(KH):
                    for u in range(SUB):
                        ins = nc.tensor.transpose(ps_x[:, k * T + u * P:k * T + (u + 1) * P],
                                                  xg[:, slot, u, k * P:(k + 1) * P], ident[:, :])
                ins.then_inc(s_xp, 1)

            def weights_at(i):
                return pe.value_load(etile[0:1, bass.ds(i, 1)], min_val=0, max_val=E - 1) * WE

            def layer(w, first, chunks, parts, banks, signal):
                hi, lo = parts
                for m in range(KM):
                    for k in range(chunks):
                        at_w = first + k * M + m * P
                        cols = slice(k * T, (k + 1) * T)
                        for n, (wp, xp) in enumerate(((w_hi, hi), (w_hi, lo), (w_lo, hi))):
                            ins = nc.tensor.matmul(
                                banks[m // 2][:, (m % 2) * T:(m % 2 + 1) * T], wp[:, bass.ds(w + at_w, P)],
                                xp[:, cols], start=(k == 0 and n == 0), stop=(k == chunks - 1 and n == 2))
                    if m % 2:
                        ins.then_inc(signal, 1)

            def layer1(i, w):
                pe.wait_ge(s_xs, i + 1)
                layer(w, W1_AT, KH, (xt_hi, xt_lo), ps_h[0], s_l1)

            def layer2(i, w):
                pe.wait_ge(s_h1, 2 * i + 2)
                layer(w, W2_AT, KM, (h1_hi, h1_lo), ps_h[1], s_l2)

            def layer3(i, w):
                pe.wait_ge(s_h2, 2 * i + 2)
                pe.wait_ge(s_y32, i + 1)
                for u in range(SUB):
                    for k in range(KM):
                        cols = slice(k * T + u * P, k * T + (u + 1) * P)
                        for n, (hp, wp) in enumerate(((h2_hi, w_hi), (h2_hi, w_lo), (h2_lo, w_hi))):
                            ins = nc.tensor.matmul(
                                ps_y[:, u * H:(u + 1) * H], hp[:, cols],
                                wp[:, bass.ds(w + (W3_AT + k * H), H)],
                                start=(k == 0 and n == 0), stop=(k == KM - 1 and n == 2))
                ins.then_inc(s_l3, 1)

            def step(i, s, turn, next1=True, next2=True):
                w = weights_at(i)
                layer2(i, w)
                if next1:
                    layer1(i + 1, weights_at(i + 1))
                if next2:
                    transpose_x(i + 2, (s + 2) % RING, turn + (s + 2) // RING + 1)
                layer3(i, w)

            pe.wait_ge(s_ready, 1)
            transpose_x(0, 0, 1)
            layer1(0, weights_at(0))
            transpose_x(1, 1, 1)
            with pe.Fori(0, GROUPS - 1, 1) as g:
                for s in range(RING):
                    step(g * RING + s, s, g)
            for s in range(RING):
                i = TILES - RING + s
                step(i, s, GROUPS - 1, i + 1 < TILES, i + 2 < TILES)


def kernel(x, cond_256, L0_cond_rms_w, L0_cond_wg_W, L0_cond_wg_b, L0_cond_gg_W, L0_cond_gg_b,
           L0_cond_W1, L0_cond_b1, L0_cond_W2, L0_cond_b2, L0_cond_W3, L0_cond_b3):
    import numpy as np
    import concourse.bacc as bacc
    from concourse.bass_utils import run_bass_kernel_spmd

    def chunked(w):
        return w.reshape(w.shape[0] // P, P, w.shape[1]).transpose(1, 0, 2).reshape(P, -1)

    x = np.asarray(x)
    w1, w2, w3 = (np.asarray(w) for w in (L0_cond_W1, L0_cond_W2, L0_cond_W3))
    chunks = []
    for e in range(E):
        chunks.append(np.concatenate([chunked(w1[e]), chunked(w3[e])], axis=1))
        chunks.append(chunked(w2[e]))
    arrays = {
        "x": x.reshape(N, H),
        "condT": np.repeat(np.asarray(cond_256).T, P // x.shape[0], axis=1),
        "rms_w": np.asarray(L0_cond_rms_w).reshape(KH, P).T,
        "wg": np.asarray(L0_cond_wg_W).reshape(KH, P, E).transpose(1, 0, 2),
        "gate_b": np.stack([np.asarray(L0_cond_wg_b), np.asarray(L0_cond_gg_b)]),
        "gg_W": np.asarray(L0_cond_gg_W),
        "weights": np.stack(chunks),
        "b1": np.asarray(L0_cond_b1).reshape(E, KM, P).transpose(2, 0, 1),
        "b2": np.asarray(L0_cond_b2).reshape(E, KM, P).transpose(2, 0, 1),
        "b3": np.asarray(L0_cond_b3),
    }
    arrays = {name: np.ascontiguousarray(a) for name, a in arrays.items()}
    nc = bacc.Bacc("TRN2", target_bir_lowering=False, num_devices=1)
    args = [nc.dram_tensor(f"in_{name}", a.shape, F32, kind="ExternalInput").ap() for name, a in arrays.items()]
    out = nc.dram_tensor("out", (N, H), F32, kind="ExternalOutput").ap()
    build_moe(nc, *args, out)
    got = run_bass_kernel_spmd(nc, [{f"in_{name}": a for name, a in arrays.items()}], core_ids=[0])
    return got.results[0]["out"].reshape(x.shape)
```

```python
from contextlib import ExitStack

import concourse.bass as bass
from concourse import mybir

ALU = mybir.AluOpType
ACT = mybir.ActivationFunctionType
AX = mybir.AxisListType
RED = bass.bass_isa.ReduceOp
F32 = mybir.dt.float32
F16 = mybir.dt.float16
I32 = mybir.dt.int32
U32 = mybir.dt.uint32

P = 128
E = 8
H = 256
M = 512
N = 4096
J = N // P
G = 64
KH = H // P
KM = M // P
T = 256
SUB = T // P
TILES = (2 * N - E) // T + E
COLS = TILES * SUB
MAXT = N // T
RING = 3
GROUPS = TILES // RING
assert TILES % RING == 0
CHUNK = 2048
CHUNKS = 2 * E
WE = 2 * CHUNK
W1_AT, W3_AT, W2_AT = 0, KH * M, KH * M + KM * H
STAGES = 3
PRM = 12 + H
TOP = float(2.0 ** 15)
WSCALE = float(2.0 ** 14)
EXPONENT = 0x7F800000
EPS = 1e-6
FAR = 1 << 20
RR = 8
HALF = CHUNK // 2
EARLY = 8
LATE = {0: (8,), 1: (9, 10), 2: (11,), 3: (12, 13), 4: (14,), 5: (15,)}
PEELED = len(LATE)
assert PEELED % RING == 0
EXP_AFTER = 3
CHUNKS_AT = {9: 4, 20: 5, 34: 6, 48: 7}
Q4 = J // 4


def build_moe(nc, x, small_in, cond_in, weights, b3, out):
    with ExitStack() as ctx:
        def sb(name, shape, dt):
            return ctx.enter_context(nc.sbuf_tensor(name, shape, dt))

        def sem(name):
            return ctx.enter_context(nc.semaphore(name))

        w_hi = sb("w_hi", [P, E * WE], F16)
        w_lo = sb("w_lo", [P, E * WE], F16)
        stage = sb("stage", [P, STAGES, CHUNK], F32)
        prm = sb("prm", [P, E, PRM], F32)
        area = sb("area", [P, J * H], F32)
        ident = sb("ident", [P, P], F32)
        tab_from = sb("tab_from", [P, COLS], I32)
        tab_to = sb("tab_to", [P, COLS], I32)
        tab_w = sb("tab_w", [P, COLS], F32)
        etile = sb("etile", [P, TILES], I32)
        cfrom = sb("cfrom", [P, RING, SUB], I32)
        cto = sb("cto", [P, RING, SUB], I32)
        cw = sb("cw", [P, RING, SUB], F32)
        cprm = sb("cprm", [P, RING, PRM], F32)
        before = sb("before", [P, P], F16)
        ones16 = sb("ones16", [P, P], F16)
        iota_r = sb("iota_r", [P, P], F16)
        iota_c = sb("iota_c", [P, COLS], F16)
        shared = sb("shared", [P, 1536], F32)
        packed = sb("packed", [P, KH + KH * E + 2 * E * KM], F32)
        rmsw = packed[:, 0:KH]
        wg_in = packed[:, KH:KH + KH * E].rearrange("p (k e) -> p k e", k=KH)
        bias_in = packed[:, KH + KH * E:].rearrange("p (e c) -> p e c", e=E)
        wgs = sb("wgs", [P, KH, E], F32)
        cond_g = sb("cond_g", [G + 2, P + E], F32)
        cond_s, ggw_s = cond_g[:, 0:P], cond_g[:, P:P + E]
        sel_f = sb("sel_f", [P, 64], F32)
        ssq = sb("ssq", [P, J], F32)
        var = sb("var", [P, J], F32)[:, :]
        rstd = sb("rstd", [P, J], F32)[:, :]
        wsq = sb("wsq", [P, CHUNKS, 2], F32)
        fsq = sb("fsq", [P, CHUNKS, 2], F32)
        fpow = sb("fpow", [P, CHUNKS, 2], F32)
        scale = sb("scale", [P, E, 5], F32)
        inv_scale = sb("inv_scale", [P, E, 5], F32)
        bound = sb("bound", [P, E, 2], F32)
        bpow = sb("bpow", [P, E, 2], F32)
        halves = sb("halves", [P, J], F32)
        rank = sb("rank", [P, E], F32)
        small = sb("small", [P, 7, 16], F32)
        tokv = sb("tokv", [P, J], F32)
        k_tile = sb("k_tile", [P, MAXT], F32)
        i_tile = sb("i_tile", [P, TILES], F32)
        part, whole = small[:, 0, :], small[:, 1, :]
        xmax, xmax_all = small[:, 2, 0:1], small[:, 3, 0:1]
        xpow = small[:, 4, 2:3]
        sx, inv_sx = small[:, 4, 0:1], small[:, 4, 1:2]
        ntile, tend = small[:, 5, 0:E], small[:, 5, E:2 * E]
        ones8 = small[:, 6, 0:E]

        at = [0]

        def take(cols):
            at[0] += cols
            return area[:, at[0] - cols:at[0]]

        h1_32, h2_32 = take(KM * T), take(KM * T)
        h1_hi, h1_lo, h2_hi, h2_lo = (take(KM * T // 2).bitcast(F16) for _ in range(4))
        xg = take(RING * SUB * H).rearrange("p (s u h) -> p s u h", s=RING, u=SUB)
        xt_hi, xt_lo = (take(KH * T // 2).bitcast(F16) for _ in range(2))
        y32 = take(SUB * H)
        yb = take(RING * SUB * H).rearrange("p (s u h) -> p s u h", s=RING, u=SUB)
        assert at[0] == J * H
        x_sb = area[:, :].rearrange("p (j h) -> p j h", j=J)

        at[0] = 0
        gate, cand, oh1, oh2, total, upto, restart = (take(E * J) for _ in range(7))
        second = take(E * J)
        ex = take(E * J + J)
        sel16 = take(E * J // 2).bitcast(F16)
        cmp_n = take(E * MAXT)
        cmp_t = take(TILES * E)
        et_f = take(TILES)
        cand_ex = take(E * J + J)
        tmp, m1, m2, r1, rs = (take(J) for _ in range(5))
        genre = take(E)
        slot_f = take(2 * J)
        slot_i = take(2 * J).bitcast(I32)
        part_i = take(2 * J).bitcast(I32)
        col_f, row_f = take(2 * J), take(2 * J)
        wt = take(2 * J)
        wt16 = take(J).bitcast(F16)
        wt_h, wt_l = take(2 * J), take(2 * J)
        code, pad, pos_f = take(COLS), take(COLS), take(COLS)
        wsum = take(COLS)
        assert at[0] <= J * H

        def chunk_scale(q, a):
            which = 2 if q % 2 else a
            return scale[:, q // 2, which:which + 1]

        def unread(first, n):
            return w_lo[:, first:first + n].bitcast(mybir.dt.bfloat16)

        def ej(ap):
            return ap.rearrange("p (e j) -> p e j", e=E)

        def je(ap):
            return ap.rearrange("p (e j) -> p j e", e=E)

        def over_j(ap):
            return ap.unsqueeze(2).to_broadcast([P, E, J])

        def over_e(ap):
            return ap.unsqueeze(1).to_broadcast([P, E, J])

        xT = shared[:, :].rearrange("p (r c) -> p r c", r=3)
        gates_t = w_lo[0:E, 8 * CHUNK:8 * CHUNK + 2 * N].bitcast(F32)
        hot_r = shared[:, 0:RR * P // 2].bitcast(F16).rearrange("p (r c) -> p r c", r=RR)
        q_at = RR * P // 2
        hot_q = shared[:, q_at:q_at + RR * 3 * COLS // 2].bitcast(F16)\
            .rearrange("p (r v c) -> p r v c", r=RR, v=3)
        assert q_at + RR * 3 * COLS // 2 <= 1536

        bank = [ctx.enter_context(nc.psum_tensor(f"bank{b}", [P, 512], F32)) for b in range(7)]
        ps_gate, ps_genre = bank[6][:, 0:E * J], bank[6][:, E * J:E * J + E]
        ps_before, ps_total = bank[4][:, 0:E * J], bank[4][:, E * J:2 * E * J]
        ps_slots = bank[3][:, 0:3 * COLS]
        ps_h = [[bank[0], bank[1]], [bank[2], bank[3]]]
        ps_x, ps_y = bank[4], bank[5]

        s_const = sem("s_const")
        s_cid = sem("s_cid")
        s_small = sem("s_small")
        s_x = [sem(f"s_x{c}") for c in range(4)]
        s_w = [sem(f"s_w{c}") for c in range(STAGES)]
        s_out0 = sem("s_out0")
        s_b3 = sem("s_b3")
        s_wgs = sem("s_wgs")
        s_xtp = sem("s_xtp")
        s_xts = sem("s_xts")
        s_gmm = sem("s_gmm")
        s_gts = sem("s_gts")
        s_gate = sem("s_gate")
        s_ssq = sem("s_ssq")
        s_var = sem("s_var")
        s_pow = sem("s_pow")
        s_wsq = sem("s_wsq")
        s_pool = sem("s_pool")
        s_wpow = sem("s_wpow")
        s_wsc = sem("s_wsc")
        s_whi = sem("s_whi")
        s_wlo = sem("s_wlo")
        s_dve = sem("s_dve")
        s_diff = sem("s_diff")
        s_exp = sem("s_exp")
        s_sel = sem("s_sel")
        s_cnt = sem("s_cnt")
        s_hot = sem("s_hot")
        s_inv = sem("s_inv")
        s_norm = sem("s_norm")
        s_xpow = sem("s_xpow")
        s_sx = sem("s_sx")
        s_bpow = sem("s_bpow")
        s_inverse = sem("s_inverse")
        s_tab = sem("s_tab")
        s_own = sem("s_own")
        s_idx = sem("s_idx")
        s_prm = sem("s_prm")
        s_cw = sem("s_cw")
        s_xg = [sem(f"s_xg{s}") for s in range(RING)]
        s_xp = sem("s_xp")
        s_xhi = sem("s_xhi")
        s_xs = sem("s_xs")
        s_l1 = sem("s_l1")
        s_h1f = sem("s_h1f")
        s_h1h = sem("s_h1h")
        s_h1 = sem("s_h1")
        s_l2 = sem("s_l2")
        s_h2f = sem("s_h2f")
        s_h2h = sem("s_h2h")
        s_h2 = sem("s_h2")
        s_l3 = sem("s_l3")
        s_y32 = sem("s_y32")
        s_y = sem("s_y")
        s_add = sem("s_add")

        block = ctx.enter_context(nc.Block())

        @block.sync
        def _(sp):
            for c in range(4):
                js = J // 4
                sp.dma_start(area[:, c * js * H:(c + 1) * js * H],
                             x.rearrange("(p j) h -> p (j h)", p=P)[:, c * js * H:(c + 1) * js * H])\
                  .then_inc(s_x[c], 16)
            for q in range(CHUNKS):
                if q >= STAGES:
                    sp.wait_ge(s_wlo, 2 * (q - STAGES + 1))
                sp.dma_start(stage[:, q % STAGES, :], weights[q]).then_inc(s_w[q % STAGES], 16)
                if q == STAGES - 1:
                    sp.dma_start(prm[:, :, 12:PRM], b3.unsqueeze(0).to_broadcast([P, E, H])).then_inc(s_b3, 16)
                    sp.dma_start(out, x).then_inc(s_out0, 16)

        @block.gpsimd
        def _(pool):
            chain = [0]

            def link(ins):
                chain[0] += 1
                ins.then_inc(s_pool, 1)
                pool.wait_ge(s_pool, chain[0])

            link(pool.memset(ident[:, :], 0.0))
            pool.affine_select(out=ident[:, :], in_=ident[:, :], compare_op=ALU.not_equal, fill=1.0,
                               base=0, pattern=[[-1, P]], channel_multiplier=1).then_inc(s_cid, 1)
            link(pool.memset(halves[:, :], -0.5))
            pool.memset(ones16[:, :], 1.0).then_inc(s_const, 1)
            link(pool.memset(before[:, :], 1.0))
            pool.affine_select(out=before[:, :], in_=before[:, :], compare_op=ALU.is_gt, fill=0.0,
                               base=0, pattern=[[1, P]], channel_multiplier=-1).then_inc(s_const, 1)
            pool.iota(iota_r[:, :], pattern=[[1, P]], base=0, channel_multiplier=0,
                      allow_small_or_imprecise_dtypes=True).then_inc(s_const, 1)
            pool.iota(iota_c[:, :], pattern=[[1, COLS]], base=0, channel_multiplier=0,
                      allow_small_or_imprecise_dtypes=True).then_inc(s_const, 1)
            pool.iota(rank[:, :], pattern=[[-1, E]], base=E, channel_multiplier=0,
                      allow_small_or_imprecise_dtypes=True).then_inc(s_const, 1)

            def weight_norms(q):
                pool.wait_ge(s_wsq, 2 * q + 2)
                w = 2
                if q % 2:
                    link(pool.tensor_tensor(wsq[:, q, 0:1], wsq[:, q, 0:1], wsq[:, q, 1:2], ALU.add))
                    w = 1
                link(pool.partition_all_reduce(fsq[:, q, 0:w], wsq[:, q, 0:w], P, RED.add))
                link(pool.tensor_scalar(fpow[:, q, 0:w], fsq[:, q, 0:w], 1e-30, TOP ** -2, ALU.max, ALU.mult))
                pool.tensor_tensor(fpow[:, q, 0:w], fpow[:, q, 0:w], halves[:, 0:w], ALU.pow)\
                    .then_inc(s_wpow, 1)

            pool.iota(tokv[:, :], pattern=[[1, J]], base=-N // 2, channel_multiplier=J,
                      allow_small_or_imprecise_dtypes=True).then_inc(s_const, 1)
            pool.iota(k_tile[:, :], pattern=[[T, MAXT]], base=0, channel_multiplier=0,
                      allow_small_or_imprecise_dtypes=True).then_inc(s_const, 1)
            pool.iota(i_tile[:, :], pattern=[[1, TILES]], base=0, channel_multiplier=0,
                      allow_small_or_imprecise_dtypes=True).then_inc(s_const, 1)

            def bounds(e):
                one, two = bound[:, e, 0:1], bound[:, e, 1:2]
                link(pool.tensor_scalar(one, fsq[:, 2 * e, 0:1], xmax_all, whole[:, e:e + 1], ALU.mult, ALU.add))
                link(pool.tensor_scalar(two, one, fsq[:, 2 * e + 1, 0:1], whole[:, E + e:E + e + 1],
                                        ALU.mult, ALU.add))
                link(pool.tensor_scalar(bound[:, e, :], bound[:, e, :], 1e-30, 4 * TOP ** -2, ALU.max, ALU.mult))
                pool.tensor_tensor(bpow[:, e, :], bound[:, e, :], halves[:, 0:2], ALU.pow).then_inc(s_bpow, 1)

            def parameters(e):
                pool.wait_ge(s_inverse, e + 1)
                sc, inv = scale[:, e, :], inv_scale[:, e, :]
                pool.tensor_scalar(prm[:, e, 0:1], sc[:, 3:4], inv_sx, inv[:, 0:1], ALU.mult, ALU.mult)
                pool.tensor_scalar(prm[:, e, 1:2], sc[:, 4:5], inv[:, 3:4], inv[:, 2:3], ALU.mult, ALU.mult)
                pool.tensor_scalar(prm[:, e, 2:3], inv[:, 4:5], inv[:, 1:2], None, ALU.mult)
                pool.tensor_scalar(prm[:, e, 4:8], prm[:, e, 4:8], sc[:, 3:4], None, ALU.mult)
                link(pool.tensor_scalar(prm[:, e, 8:12], prm[:, e, 8:12], sc[:, 4:5], None, ALU.mult))

            for c in range(4):
                pool.wait_ge(s_var, c + 1)
                js = slice(c * J // 4, (c + 1) * J // 4)
                pool.tensor_tensor(rstd[:, js], var[:, js], halves[:, js], ALU.pow).then_inc(s_pow, 1)
            pool.wait_ge(s_norm, 1)
            pool.partition_all_reduce(xmax_all, xmax, P, RED.max)
            link(pool.partition_all_reduce(whole, part, P, RED.add))
            link(pool.tensor_scalar(xpow, xmax_all, 1e-30, TOP ** -2, ALU.max, ALU.mult))
            pool.tensor_tensor(xpow, xpow, halves[:, 0:1], ALU.pow).then_inc(s_xpow, 1)
            pool.wait_ge(s_sx, 1)
            link(pool.memset(prm[:, :, 3:4], 0.0))
            for e in range(EARLY // 2):
                weight_norms(2 * e)
                weight_norms(2 * e + 1)
                bounds(e)
                parameters(e)

            pool.wait_ge(s_tab, 1)
            pool.wait_ge(s_b3, 16)
            def copy_columns(to, table, i, signal):
                pool.tensor_copy(to, table[:, bass.ds(i * SUB, SUB)]).then_inc(signal, 1)

            def gather(i, s, copied):
                pool.wait_ge(s_idx, copied)
                pool.sem_inc(s_own, 1)
                for u in range(SUB):
                    pool.indirect_dma_start(
                        out=xg[:, s, u, :], out_offset=None, in_=x,
                        in_offset=bass.IndirectOffsetOnAxis(ap=cfrom[:, s, u:u + 1].bitcast(U32), axis=0),
                    ).then_inc(s_xg[s], 16)

            def copy_parameters(i, s):
                e = pool.value_load(etile[0:1, bass.ds(i, 1)], min_val=0, max_val=E - 1)
                pool.tensor_copy(cprm[:, s, :], prm[:, :, :].rearrange("p e c -> p (e c)")
                                 [:, bass.ds(e * PRM, PRM)]).then_inc(s_prm, 1)

            def add_rows(i, s):
                for u in range(SUB):
                    pool.indirect_dma_start(
                        out=out, out_offset=bass.IndirectOffsetOnAxis(ap=cto[:, s, u:u + 1].bitcast(U32), axis=0),
                        in_=yb[:, s, u, :], in_offset=None, bounds_check=N - 1, oob_is_err=False,
                        compute_op=ALU.add,
                    ).then_inc(s_add, 16)

            def step(i, s, first=False, late=(), next2=True, next3=True):
                s2 = (s + 2) % RING
                copy_columns(cto[:, s, :], tab_to, i, s_idx)
                if next3:
                    pool.wait_ge(s_xp, i + 1)
                    copy_columns(cfrom[:, s, :], tab_from, i + 3, s_idx)
                    gather(i + 3, s, RING + 2 * i + 2)
                else:
                    last = TILES - RING
                    pool.wait_ge(s_idx, RING + 2 * last + (i - last) + 1)
                for q in late:
                    weight_norms(q)
                    if q % 2:
                        bounds(q // 2)
                        parameters(q // 2)
                if next2:
                    copy_parameters(i + 2, s2)
                pool.wait_ge(s_y, 2 * i + 3)
                pool.sem_inc(s_own, 1)
                if not first:
                    pool.wait_ge(s_add, i * SUB * 16)
                    pool.sem_inc(s_own, 1)
                if next2:
                    copy_columns(cw[:, s2, :], tab_w, i + 2, s_cw)
                add_rows(i, s)

            for i in range(RING):
                copy_columns(cfrom[:, i, :], tab_from, i, s_idx)
                gather(i, i, i + 1)
            for i in range(2):
                copy_parameters(i, i)
                copy_columns(cw[:, i, :], tab_w, i, s_cw)
            pool.wait_ge(s_out0, 16)
            for i in range(PEELED):
                step(i, i % RING, first=(i == 0), late=LATE[i])
            with pool.Fori(PEELED // RING, GROUPS - 1, 1) as g:
                for s in range(RING):
                    step(g * RING + s, s)
            for s in range(RING):
                i = TILES - RING + s
                step(i, s, next2=i + 2 < TILES, next3=False)
            pool.wait_ge(s_add, TILES * SUB * 16)

        @block.scalar
        def _(act):
            act.dma_start(packed[:, :], small_in).then_inc(s_small, 16)
            act.dma_start(cond_g[:, :], cond_in).then_inc(s_small, 16)

            for j in range(J):
                if j % (J // 4) == 0:
                    act.wait_ge(s_x[j // (J // 4)], 16)
                act.activation(unread(E * WE - (J - j) * H, H), x_sb[:, j, :], ACT.Square,
                               accum_out=ssq[:, j:j + 1]).then_inc(s_ssq, 1)

            def squares(q):
                act.wait_ge(s_w[q % STAGES], 16 * (q // STAGES + 1))
                for a in range(2):
                    act.activation(unread(q * CHUNK + a * HALF, HALF), stage[:, q % STAGES, a * HALF:(a + 1) * HALF], ACT.Square,
                                   accum_out=wsq[:, q, a:a + 1]).then_inc(s_wsq, 1)

            def high_parts(q):
                act.wait_ge(s_wsc, q + 1)
                for a in range(2):
                    act.activation(w_hi[:, q * CHUNK + a * HALF:q * CHUNK + (a + 1) * HALF],
                                   stage[:, q % STAGES, a * HALF:(a + 1) * HALF], ACT.Copy,
                                   scale=chunk_scale(q, a)).then_inc(s_whi, 1)

            for q in range(EARLY):
                squares(q)
                if q >= 1:
                    high_parts(q - 1)
                if q == EXP_AFTER:
                    act.wait_ge(s_diff, 1)
                    act.activation(ex, cand_ex, ACT.Exp).then_inc(s_exp, 1)
            high_parts(EARLY - 1)

            def x_high(i):
                act.wait_ge(s_xp, i + 1)
                act.activation(xt_hi, ps_x[:, :], ACT.Copy, scale=sx).then_inc(s_xhi, 1)

            def activate(i, slot, layer):
                if layer == 0:
                    act.wait_ge(s_prm, i + 1)
                done, signal, to = ((s_l1, s_h1f, h1_32), (s_l2, s_h2f, h2_32))[layer]
                for b in range(2):
                    act.wait_ge(done, 2 * i + b + 1)
                    for a in range(2):
                        m = 2 * b + a
                        act.activation(to[:, m * T:(m + 1) * T], ps_h[layer][b][:, a * T:(a + 1) * T], ACT.Relu,
                                       bias=cprm[:, slot, 4 + 4 * layer + m:5 + 4 * layer + m],
                                       scale=cprm[:, slot, layer:layer + 1]).then_inc(signal, 1)

            def weigh(i, slot):
                act.wait_ge(s_y32, i + 2)
                act.wait_ge(s_cw, i + 1)
                for u in range(SUB):
                    act.activation(yb[:, slot, u, :], y32[:, u * H:(u + 1) * H], ACT.Copy,
                                   scale=cw[:, slot, u:u + 1]).then_inc(s_y, 1)

            def step(i, s, late=(), next1=True, next2=True):
                for q in late:
                    squares(q)
                activate(i, s, 1)
                if next1:
                    activate(i + 1, (s + 1) % RING, 0)
                if next2:
                    x_high(i + 2)
                for q in late:
                    high_parts(q)
                weigh(i, s)

            act.wait_ge(s_tab, 1)
            act.sem_inc(s_y, 1)
            x_high(0)
            activate(0, 0, 0)
            x_high(1)
            for i in range(PEELED):
                step(i, i % RING, late=LATE[i])
            with act.Fori(PEELED // RING, GROUPS - 1, 1) as g:
                for s in range(RING):
                    step(g * RING + s, s)
            for s in range(RING):
                i = TILES - RING + s
                step(i, s, next1=i + 1 < TILES, next2=i + 2 < TILES)

        @block.vector
        def _(dve):
            chain = [0]

            def link(ins):
                chain[0] += 1
                ins.then_inc(s_dve, 1)
                dve.wait_ge(s_dve, chain[0])

            def weight_scales(q):
                dve.wait_ge(s_wpow, q + 1)
                e, to, w = q // 2, 2 * (q % 2), 2 - q % 2
                dve.tensor_scalar(scale[:, e, to:to + w].bitcast(I32), fpow[:, q, 0:w].bitcast(I32), EXPONENT, None,
                                  ALU.bitwise_and).then_inc(s_wsc, 1)

            def inverses(e):
                dve.wait_ge(s_bpow, e + 1)
                link(dve.tensor_scalar(scale[:, e, 3:5].bitcast(I32), bpow[:, e, :].bitcast(I32), EXPONENT, None,
                                       ALU.bitwise_and))
                dve.reciprocal(inv_scale[:, e, :], scale[:, e, :]).then_inc(s_inverse, 1)

            def low_parts(q):
                for a in range(2):
                    dve.wait_ge(s_whi, 2 * q + a + 1)
                    at_w = q * CHUNK + a * HALF
                    dve.scalar_tensor_tensor(
                        w_lo[:, at_w:at_w + HALF], stage[:, q % STAGES, a * HALF:(a + 1) * HALF],
                        chunk_scale(q, a), w_hi[:, at_w:at_w + HALF], ALU.mult, ALU.subtract).then_inc(s_wlo, 1)

            def weight_step(q):
                if q >= 2 and q % 2 == 0:
                    inverses(q // 2 - 1)
                weight_scales(q)
                if q >= 1:
                    low_parts(q - 1)

            dve.wait_ge(s_small, 2 * 16)
            for k in range(KH):
                ins = dve.tensor_scalar(wgs[:, k, :], wg_in[:, k, :], rmsw[:, k:k + 1], None, ALU.mult)
            ins.then_inc(s_wgs, 1)
            dve.tensor_copy(prm[:, :, 4:12], bias_in)
            bsq = sel_f[:, 0:64].rearrange("p (l e c) -> p l e c", l=2, e=E)
            link(dve.tensor_tensor(bsq, bias_in.rearrange("p e (l c) -> p l e c", l=2),
                                   bias_in.rearrange("p e (l c) -> p l e c", l=2), ALU.mult))
            link(dve.tensor_reduce(part.rearrange("p (l e) -> p l e", l=2), bsq, AX.X, ALU.add))
            link(dve.tensor_scalar(part[:, E:], part[:, E:], 0.5, None, ALU.mult))

            def variances(c):
                js = slice(c * J // 4, (c + 1) * J // 4)
                dve.wait_ge(s_ssq, (c + 1) * J // 4)
                dve.tensor_scalar(var[:, js], ssq[:, js], 1.0 / H, EPS, ALU.mult, ALU.add).then_inc(s_var, 1)

            def gates_out(jq):
                dve.wait_ge(s_gmm, 2 * jq + 2)
                dve.tensor_copy(gates_t[:, jq * 4 * P:(jq + 1) * 4 * P], bank[4 + jq % 2][0:E, :]).then_inc(s_gts, 1)

            for jq in range(Q4):
                for k in range(KH):
                    u = KH * jq + k
                    dve.wait_ge(s_xtp, u + 1)
                    if u >= 3:
                        dve.wait_ge(s_gmm, u - 2)
                    dve.tensor_copy(xT[:, u % 3, :], bank[u % 4][:, :]).then_inc(s_xts, 1)
                if jq >= 1:
                    gates_out(jq - 1)
                if jq >= 3 and jq % 2:
                    variances((jq - 3) // 2)
            variances(3)
            gates_out(Q4 - 1)
            dve.tensor_reduce(xmax, ssq[:, :], AX.X, ALU.max).then_inc(s_norm, 1)
            dve.wait_ge(s_gate, 1)
            dve.wait_ge(s_pow, 4)
            link(dve.tensor_tensor(tmp, rstd, rstd, ALU.mult))
            link(dve.tensor_tensor(tmp, tmp, var, ALU.mult))
            link(dve.tensor_scalar(tmp, tmp, -0.5, 1.5, ALU.mult, ALU.add))
            link(dve.tensor_tensor(rstd, rstd, tmp, ALU.mult))
            link(dve.tensor_tensor(ej(gate), ps_gate.rearrange("p (j e) -> p e j", e=E), over_e(rstd), ALU.mult))
            link(dve.tensor_copy(genre, ps_genre))
            link(dve.tensor_tensor(ej(gate), ej(gate), over_j(genre), ALU.add))
            dve.wait_ge(s_const, 8)
            link(dve.tensor_scalar(tokv[P // 2:P, :], tokv[P // 2:P, :], 1.0, None, ALU.add))

            def pick(scores, top, onehot, best):
                link(dve.tensor_reduce(top, je(scores), AX.X, ALU.max))
                link(dve.tensor_tensor(ej(cand), ej(scores), over_e(top), ALU.is_equal))
                link(dve.tensor_tensor(ej(cand), ej(cand), over_j(rank[:, :]), ALU.mult))
                link(dve.tensor_reduce(best, je(cand), AX.X, ALU.max))
                link(dve.tensor_tensor(ej(onehot), ej(cand), over_e(best), ALU.is_equal))

            pick(gate, m1, oh1, r1)
            dve.wait_ge(s_xpow, 1)
            link(dve.tensor_scalar(sx.bitcast(I32), xpow.bitcast(I32), EXPONENT, None, ALU.bitwise_and))
            dve.reciprocal(inv_sx, sx).then_inc(s_sx, 1)
            link(dve.scalar_tensor_tensor(second, oh1, -3e38, gate, ALU.mult, ALU.add))
            pick(second, m2, oh2, r1)
            dve.tensor_tensor(cand_ex[:, 0:E * J].rearrange("p (e j) -> p e j", e=E), ej(gate), over_e(m1),
                              ALU.subtract)
            dve.tensor_tensor(cand_ex[:, E * J:], m2, m1, ALU.subtract).then_inc(s_diff, 1)
            dve.tensor_tensor(sel16, oh1, oh2, ALU.add).then_inc(s_sel, 1)
            weight_step(0)
            weight_step(1)
            link(dve.memset(restart, 1.0))
            link(dve.memset(ej(restart)[:, :, 0:1], 0.0))
            dve.wait_ge(s_cnt, 1)
            link(dve.tensor_copy(total, ps_total))
            link(dve.tensor_tensor_scan(upto, restart, total, 0.0, ALU.mult, ALU.add))
            count = ej(upto)[:, :, J - 1:J]
            link(dve.tensor_tensor(cmp_n.rearrange("p (e k) -> p e k", e=E), count.to_broadcast([P, E, MAXT]),
                                   k_tile[:, :].unsqueeze(1).to_broadcast([P, E, MAXT]), ALU.is_gt))
            link(dve.tensor_reduce(ntile, cmp_n.rearrange("p (e k) -> p e k", e=E), AX.X, ALU.add))
            link(dve.tensor_scalar(ntile, ntile, 1.0, None, ALU.max))
            link(dve.memset(ones8, 1.0))
            link(dve.tensor_tensor_scan(tend, ones8, ntile, 0.0, ALU.mult, ALU.add))
            link(dve.tensor_tensor(cmp_t.rearrange("p (i e) -> p i e", e=E),
                                   i_tile[:, :].unsqueeze(2).to_broadcast([P, TILES, E]),
                                   tend.unsqueeze(1).to_broadcast([P, TILES, E]), ALU.is_ge))
            link(dve.tensor_reduce(et_f, cmp_t.rearrange("p (i e) -> p i e", e=E), AX.X, ALU.add))
            link(dve.tensor_scalar(etile[:, :], et_f, float(E - 1), None, ALU.min))
            link(dve.tensor_tensor(ntile, tend, ntile, ALU.subtract))
            link(dve.tensor_scalar(ntile, ntile, float(T), None, ALU.mult))
            link(dve.tensor_tensor(upto, upto, total, ALU.subtract))
            link(dve.tensor_tensor(upto, upto, ps_before, ALU.add))
            link(dve.tensor_tensor(ej(upto), ej(upto), over_j(ntile), ALU.add))
            for k, oh in enumerate((oh1, oh2)):
                link(dve.tensor_tensor(cand, oh, upto, ALU.mult))
                link(dve.tensor_reduce(slot_f[:, k * J:(k + 1) * J], je(cand), AX.X, ALU.add))
            link(dve.tensor_copy(slot_i, slot_f))
            link(dve.tensor_scalar(part_i, slot_i, P - 1, None, ALU.bitwise_and))
            link(dve.tensor_copy(row_f, part_i))
            link(dve.tensor_scalar(slot_i, slot_i, P.bit_length() - 1, None, ALU.logical_shift_right))
            link(dve.tensor_copy(col_f, slot_i))
            weight_step(2)
            weight_step(3)
            dve.wait_ge(s_exp, 1)
            link(dve.tensor_reduce(rs, je(ex[:, 0:E * J]), AX.X, ALU.add))
            link(dve.reciprocal(rs, rs))
            link(dve.tensor_scalar(wt[:, 0:J], rs, WSCALE, None, ALU.mult))
            link(dve.tensor_tensor(wt[:, J:2 * J], ex[:, E * J:], wt[:, 0:J], ALU.mult))
            link(dve.tensor_copy(wt16, wt))
            link(dve.tensor_copy(wt_h, wt16))
            link(dve.tensor_tensor(wt_l, wt, wt_h, ALU.subtract))
            for n in range(2 * J):
                if n >= RR:
                    dve.wait_ge(s_inv, n - RR + 1)
                dve.tensor_scalar(hot_r[:, n % RR, :], iota_r[:, :], row_f[:, n:n + 1], None, ALU.is_equal)
                for v, val in enumerate((tokv[:, n % J:n % J + 1], wt_h[:, n:n + 1], wt_l[:, n:n + 1])):
                    ins = dve.tensor_scalar(hot_q[:, n % RR, v, :], iota_c[:, :], col_f[:, n:n + 1], val,
                                            ALU.is_equal, ALU.mult)
                ins.then_inc(s_hot, 1)
                if n in CHUNKS_AT:
                    weight_step(CHUNKS_AT[n])
            dve.wait_ge(s_inv, 2 * J)
            inv = ps_slots.rearrange("p (v c) -> p v c", v=3)
            link(dve.tensor_copy(code, inv[:, 0, :]))
            link(dve.tensor_scalar(pos_f, code, 0.0, None, ALU.is_gt))
            link(dve.tensor_scalar(pad, code, 0.0, float(FAR), ALU.is_equal, ALU.mult))
            link(dve.scalar_tensor_tensor(code, code, float(N // 2), pos_f, ALU.add, ALU.subtract))
            dve.tensor_copy(tab_from[:, :], code)
            dve.tensor_tensor(tab_to[:, :], code, pad, ALU.add)
            link(dve.tensor_copy(wsum, inv[:, 2, :]))
            link(dve.tensor_tensor(wsum, wsum, inv[:, 1, :], ALU.add))
            dve.tensor_scalar(tab_w[:, :], wsum, 1.0 / WSCALE, None, ALU.mult).then_inc(s_tab, 1)
            low_parts(EARLY - 1)
            inverses(EARLY // 2 - 1)

            def x_low(i):
                dve.wait_ge(s_xhi, i + 1)
                dve.scalar_tensor_tensor(xt_lo, ps_x[:, :], sx, xt_hi, ALU.mult, ALU.subtract).then_inc(s_xs, 1)

            def split(i, layer):
                full, half_done, signal = ((s_h1f, s_h1h, s_h1), (s_h2f, s_h2h, s_h2))[layer]
                h, hi, lo = ((h1_32, h1_hi, h1_lo), (h2_32, h2_hi, h2_lo))[layer]
                for b in range(2):
                    cols = slice(b * 2 * T, (b + 1) * 2 * T)
                    dve.wait_ge(full, 4 * i + 2 * b + 2)
                    dve.tensor_copy(hi[:, cols], h[:, cols]).then_inc(half_done, 1)
                    dve.wait_ge(half_done, 2 * i + b + 1)
                    dve.tensor_tensor(lo[:, cols], h[:, cols], hi[:, cols], ALU.subtract).then_inc(signal, 1)

            def finish(i, slot):
                dve.wait_ge(s_l3, i + 1)
                dve.wait_ge(s_y, 2 * i + 1)
                dve.scalar_tensor_tensor(
                    y32.rearrange("p (u h) -> p u h", u=SUB), ps_y[:, :].rearrange("p (u h) -> p u h", u=SUB),
                    cprm[:, slot, 2:3], cprm[:, slot, 12:PRM].unsqueeze(1).to_broadcast([P, SUB, H]),
                    ALU.mult, ALU.add).then_inc(s_y32, 1)

            def step(i, s, late=(), next1=True, next2=True):
                split(i, 1)
                for q in late:
                    weight_scales(q)
                    if q % 2:
                        inverses(q // 2)
                if next1:
                    split(i + 1, 0)
                if next2:
                    x_low(i + 2)
                for q in late:
                    low_parts(q)
                finish(i, s)

            dve.sem_inc(s_y32, 1)
            x_low(0)
            split(0, 0)
            x_low(1)
            for i in range(PEELED):
                step(i, i % RING, late=LATE[i])
            with dve.Fori(PEELED // RING, GROUPS - 1, 1) as g:
                for s in range(RING):
                    step(g * RING + s, s)
            for s in range(RING):
                i = TILES - RING + s
                step(i, s, next1=i + 1 < TILES, next2=i + 2 < TILES)

        @block.tensor
        def _(pe):
            def transposes(jq):
                if jq % 2 == 0:
                    pe.wait_ge(s_x[jq // 2], 16)
                for k in range(KH):
                    u = KH * jq + k
                    if u >= 4:
                        pe.wait_ge(s_xts, u - 3)
                    for d in range(4):
                        ins = nc.tensor.transpose(bank[u % 4][:, d * P:(d + 1) * P],
                                                  x_sb[:, 4 * jq + d, k * P:(k + 1) * P], ident[:, :])
                    ins.then_inc(s_xtp, 1)

            def gates(jq):
                if jq >= 2:
                    pe.wait_ge(s_gts, jq - 1)
                for k in range(KH):
                    u = KH * jq + k
                    pe.wait_ge(s_xts, u + 1)
                    nc.tensor.matmul(bank[4 + jq % 2][0:E, :], wgs[:, k, :], xT[:, u % 3, :],
                                     start=(k == 0), stop=(k == KH - 1)).then_inc(s_gmm, 1)

            pe.wait_ge(s_cid, 1)
            transposes(0)
            pe.wait_ge(s_wgs, 1)
            for jq in range(1, Q4):
                transposes(jq)
                gates(jq - 1)
            gates(Q4 - 1)
            nc.tensor.matmul(ps_genre, cond_s, ggw_s, start=True, stop=True)
            for j in range(J):
                if j % 4 == 0:
                    pe.wait_ge(s_gts, j // 4 + 1)
                ins = nc.tensor.transpose(ps_gate[:, j * E:(j + 1) * E], gates_t[:, j * P:(j + 1) * P],
                                          ident[0:E, 0:E])
            ins.then_inc(s_gate, 1)
            pe.wait_ge(s_const, 8)
            pe.wait_ge(s_sel, 1)
            nc.tensor.matmul(ps_before, before[:, :], sel16, start=True, stop=True)
            nc.tensor.matmul(ps_total, ones16[:, :], sel16, start=True, stop=True).then_inc(s_cnt, 1)
            for n in range(2 * J):
                pe.wait_ge(s_hot, n + 1)
                nc.tensor.matmul(ps_slots, hot_r[:, n % RR, :], hot_q[:, n % RR, :, :].rearrange("p v c -> p (v c)"),
                                 start=(n == 0), stop=(n == 2 * J - 1)).then_inc(s_inv, 1)

            def transpose_x(i, slot, turn):
                pe.wait_ge(s_xg[slot], turn * SUB * 16)
                if not (isinstance(i, int) and i == 0):
                    pe.wait_ge(s_xs, i)
                for k in range(KH):
                    for u in range(SUB):
                        ins = nc.tensor.transpose(ps_x[:, k * T + u * P:k * T + (u + 1) * P],
                                                  xg[:, slot, u, k * P:(k + 1) * P], ident[:, :])
                ins.then_inc(s_xp, 1)

            def weights_at(i):
                return pe.value_load(etile[0:1, bass.ds(i, 1)], min_val=0, max_val=E - 1) * WE

            def layer(w, first, chunks, parts, banks, signal):
                hi, lo = parts
                for m in range(KM):
                    for k in range(chunks):
                        at_w = first + k * M + m * P
                        cols = slice(k * T, (k + 1) * T)
                        for n, (wp, xp) in enumerate(((w_hi, hi), (w_hi, lo), (w_lo, hi))):
                            ins = nc.tensor.matmul(
                                banks[m // 2][:, (m % 2) * T:(m % 2 + 1) * T], wp[:, bass.ds(w + at_w, P)],
                                xp[:, cols], start=(k == 0 and n == 0), stop=(k == chunks - 1 and n == 2))
                    if m % 2:
                        ins.then_inc(signal, 1)

            def layer1(i, w):
                if isinstance(i, int):
                    pe.wait_ge(s_wlo, 4 * min(i + 1, E))
                pe.wait_ge(s_xs, i + 1)
                layer(w, W1_AT, KH, (xt_hi, xt_lo), ps_h[0], s_l1)

            def layer2(i, w):
                pe.wait_ge(s_h1, 2 * i + 2)
                layer(w, W2_AT, KM, (h1_hi, h1_lo), ps_h[1], s_l2)

            def layer3(i, w):
                pe.wait_ge(s_h2, 2 * i + 2)
                pe.wait_ge(s_y32, i + 1)
                for u in range(SUB):
                    for k in range(KM):
                        cols = slice(k * T + u * P, k * T + (u + 1) * P)
                        for n, (hp, wp) in enumerate(((h2_hi, w_hi), (h2_hi, w_lo), (h2_lo, w_hi))):
                            ins = nc.tensor.matmul(
                                ps_y[:, u * H:(u + 1) * H], hp[:, cols],
                                wp[:, bass.ds(w + (W3_AT + k * H), H)],
                                start=(k == 0 and n == 0), stop=(k == KM - 1 and n == 2))
                ins.then_inc(s_l3, 1)

            def step(i, s, turn, next1=True, next2=True):
                w = weights_at(i)
                layer2(i, w)
                if next1:
                    layer1(i + 1, weights_at(i + 1))
                if next2:
                    transpose_x(i + 2, (s + 2) % RING, turn + (s + 2) // RING + 1)
                layer3(i, w)

            pe.wait_ge(s_tab, 1)
            transpose_x(0, 0, 1)
            layer1(0, weights_at(0))
            transpose_x(1, 1, 1)
            for i in range(PEELED):
                step(i, i % RING, i // RING)
            pe.wait_ge(s_wlo, 4 * E)
            with pe.Fori(PEELED // RING, GROUPS - 1, 1) as g:
                for s in range(RING):
                    step(g * RING + s, s, g)
            for s in range(RING):
                i = TILES - RING + s
                step(i, s, GROUPS - 1, next1=i + 1 < TILES, next2=i + 2 < TILES)


def kernel(x, cond_256, L0_cond_rms_w, L0_cond_wg_W, L0_cond_wg_b, L0_cond_gg_W, L0_cond_gg_b,
           L0_cond_W1, L0_cond_b1, L0_cond_W2, L0_cond_b2, L0_cond_W3, L0_cond_b3):
    import numpy as np
    import concourse.bacc as bacc
    from concourse.bass_utils import run_bass_kernel_spmd

    def chunked(w):
        return w.reshape(w.shape[0] // P, P, w.shape[1]).transpose(1, 0, 2).reshape(P, -1)

    x = np.asarray(x)
    w1, w2, w3 = (np.asarray(w) for w in (L0_cond_W1, L0_cond_W2, L0_cond_W3))
    chunks = []
    for e in range(E):
        chunks.append(np.concatenate([chunked(w1[e]), chunked(w3[e])], axis=1))
        chunks.append(chunked(w2[e]))
    x_rows = x.reshape(N, H)
    packed = np.concatenate([
        np.asarray(L0_cond_rms_w).reshape(KH, P).T,
        np.asarray(L0_cond_wg_W).reshape(KH, P, E).transpose(1, 0, 2).reshape(P, -1),
        np.stack([np.asarray(b).reshape(E, KM, P) for b in (L0_cond_b1, L0_cond_b2)], axis=1)
        .transpose(3, 0, 1, 2).reshape(P, -1)], axis=1)
    cond = np.concatenate([
        np.concatenate([np.repeat(np.asarray(cond_256).T, P // x.shape[0], axis=1), np.asarray(L0_cond_gg_W)], axis=1),
        np.concatenate([np.ones((2, P), x.dtype),
                        np.stack([np.asarray(L0_cond_wg_b), np.asarray(L0_cond_gg_b)])], axis=1)])
    arrays = {"x": x_rows, "small_in": packed, "cond_in": cond, "weights": np.stack(chunks),
              "b3": np.asarray(L0_cond_b3)}
    arrays = {name: np.ascontiguousarray(a) for name, a in arrays.items()}
    nc = bacc.Bacc("TRN2", target_bir_lowering=False, num_devices=1)
    args = [nc.dram_tensor(f"in_{name}", a.shape, F32, kind="ExternalInput").ap() for name, a in arrays.items()]
    out = nc.dram_tensor("out", (N, H), F32, kind="ExternalOutput").ap()
    build_moe(nc, *args, out)
    got = run_bass_kernel_spmd(nc, [{f"in_{name}": a for name, a in arrays.items()}], core_ids=[0])
    return got.results[0]["out"].reshape(x.shape)
```

```python
from contextlib import ExitStack

import concourse.bass as bass
from concourse import mybir

ALU = mybir.AluOpType
ACT = mybir.ActivationFunctionType
AX = mybir.AxisListType
RED = bass.bass_isa.ReduceOp
F32 = mybir.dt.float32
F16 = mybir.dt.float16
I32 = mybir.dt.int32
U32 = mybir.dt.uint32

P = 128
E = 8
H = 256
M = 512
N = 4096
J = N // P
G = 64
KH = H // P
KM = M // P
T = 256
SUB = T // P
TILES = (2 * N - E) // T + E
COLS = TILES * SUB
MAXT = N // T
RING = 3
GROUPS = TILES // RING
assert TILES % RING == 0
CHUNK = 2048
CHUNKS = 2 * E
WE = 2 * CHUNK
W1_AT, W3_AT, W2_AT = 0, KH * M, KH * M + KM * H
STAGES = 3
PRM = 12 + H
TOP_LOG = 15
WSCALE = float(2.0 ** 14)
EPS = 1e-6
FAR = 1 << 20
BATCH = 8
HALF = CHUNK // 2
EARLY = 8
FILL = 10
LATE = {i: FILL + i for i in range(CHUNKS - FILL)}
PEELED = 3 * RING
assert EARLY % 2 == 0 and FILL == EARLY + 2 and len(LATE) < PEELED
assert all(2 * e + 1 < FILL or 2 * e + 1 - FILL <= e - 2 for e in range(E))
SHARED = 4
EXP_AFTER = 2
BATCH_CHUNKS = {3: 4, 5: 5}
assert sorted(BATCH_CHUNKS.values()) == [BATCH_CHUNKS[b] for b in sorted(BATCH_CHUNKS)] \
    == list(range(SHARED, SHARED + len(BATCH_CHUNKS)))
OUT_AT = (2, 2, 2, 3, 4, 5, 6, 7)
WARM_START = 24
BIAS, MANT = 127, 23
VARIANCES_AT = (1, 2, 3, 4)
XT = 4
Q4 = J // 4


def build_moe(nc, x, small_in, cond_in, weights, b3, out):
    with ExitStack() as ctx:
        def sb(name, shape, dt):
            return ctx.enter_context(nc.sbuf_tensor(name, shape, dt))

        def sem(name):
            return ctx.enter_context(nc.semaphore(name))

        w_hi = sb("w_hi", [P, E * WE], F16)
        w_lo = sb("w_lo", [P, E * WE], F16)
        stage = sb("stage", [P, STAGES, CHUNK], F32)
        prm = sb("prm", [P, E, PRM], F32)
        area = sb("area", [P, J * H], F32)
        ident = sb("ident", [P, P], F32)
        tab_from = sb("tab_from", [P, COLS], I32)
        tab_to = sb("tab_to", [P, COLS], I32)
        tab_w = sb("tab_w", [P, COLS], F32)
        etile = sb("etile", [P, TILES], I32)
        cfrom = sb("cfrom", [P, RING, SUB], I32)
        cto = sb("cto", [P, RING, SUB], I32)
        cw = sb("cw", [P, RING, SUB], F32)
        cprm = sb("cprm", [P, RING, PRM], F32)
        behind = sb("behind", [P, P], F16)
        ones16 = sb("ones16", [P, P], F16)
        iota_r = sb("iota_r", [P, T], F16)
        iota_c = sb("iota_c", [P, TILES], F16)
        packed = sb("packed", [P, KH + KH * E + 2 * E * KM], F32)
        rmsw = packed[:, 0:KH]
        wg_in = packed[:, KH:KH + KH * E].rearrange("p (k e) -> p k e", k=KH)
        bias_in = packed[:, KH + KH * E:].rearrange("p (e c) -> p e c", e=E)
        wgs = sb("wgs", [P, KH, E], F32)
        cond_g = sb("cond_g", [G + 2, P + E], F32)
        cond_s, ggw_s = cond_g[:, 0:P], cond_g[:, P:P + E]
        bias_sq = sb("bias_sq", [P, 64], F32)
        ssq = sb("ssq", [P, J], F32)
        var = sb("var", [P, J], F32)[:, :]
        rstd = sb("rstd", [P, J], F32)[:, :]
        wsq = sb("wsq", [P, CHUNKS, 2], F32)
        fsq = sb("fsq", [P, CHUNKS, 2], F32)
        expo = sb("expo", [P, E, 5], I32)
        scale = sb("scale", [P, E, 5], F32)
        inv_scale = sb("inv_scale", [P, E, 5], F32)
        bound = sb("bound", [P, E, 2], F32)
        halves = sb("halves", [P, J], F32)
        restart = sb("restart", [P, E * J], F32)
        values = sb("values", [P, 2 * J, 3], F16)
        rms_tmp = sb("rms_tmp", [P, J], F32)[:, :]
        rank = sb("rank", [P, E], F32)
        small = sb("small", [P, 7, 16], F32)
        tokv = sb("tokv", [P, J], F32)
        k_tile = sb("k_tile", [P, MAXT], F32)
        i_tile = sb("i_tile", [P, TILES], F32)
        part, whole = small[:, 0, :], small[:, 1, :]
        xmax, xmax_all = small[:, 2, 0:1], small[:, 3, 0:1]
        xmax4, xexpo = small[:, 3, 1:2], small[:, 4, 2:3].bitcast(I32)
        sx, inv_sx = small[:, 4, 0:1], small[:, 4, 1:2]
        ntile, tend = small[:, 5, 0:E], small[:, 5, E:2 * E]
        ones8, genre = small[:, 6, 0:E], small[:, 6, E:2 * E]

        at = [0]

        def take(cols):
            at[0] += cols
            return area[:, at[0] - cols:at[0]]

        h1_32, h2_32 = take(KM * T), take(KM * T)
        h1_hi, h1_lo, h2_hi, h2_lo = (take(KM * T // 2).bitcast(F16) for _ in range(4))
        xg = take(RING * SUB * H).rearrange("p (s u h) -> p s u h", s=RING, u=SUB)
        xt_hi, xt_lo = (take(KH * T // 2).bitcast(F16) for _ in range(2))
        y32 = take(SUB * H)
        yb = take(RING * SUB * H).rearrange("p (s u h) -> p s u h", s=RING, u=SUB)
        assert at[0] == J * H
        x_sb = area[:, :].rearrange("p (j h) -> p j h", j=J)

        at[0] = 0
        gate, cand, oh1, oh2, upto = (take(E * J) for _ in range(5))
        second = take(E * J)
        ex = take(E * J + J)
        sel16 = take(E * J // 2).bitcast(F16)
        cmp_n = take(E * MAXT)
        cmp_t = take(TILES * E)
        et_f = take(TILES)
        cand_ex = take(E * J + J)
        m1, m2, r1, rs = (take(J) for _ in range(4))
        slot_f = take(2 * J)
        slot_i = take(2 * J).bitcast(I32)
        part_i = take(2 * J).bitcast(I32)
        wt = take(2 * J)
        wt_h = take(2 * J)
        code, pad, pos_f, wsum = (take(COLS).rearrange("p (u t) -> p u t", u=SUB) for _ in range(4))
        tile16, row_f = take(J).bitcast(F16), take(2 * J)
        pairs = area[:, at[0]:at[0] + 2 * E * J]
        hot_c = take(BATCH * TILES).bitcast(F16).rearrange("p (r n c) -> p r n c", r=2, n=BATCH)
        hot_r = take(BATCH * T).bitcast(F16).rearrange("p (r n c) -> p r n c", r=2, n=BATCH)
        hot_q = take(3 * BATCH * TILES).bitcast(F16).rearrange("p (r n v c) -> p r n v c", r=2, n=BATCH, v=3)
        assert at[0] <= J * H

        def chunk_scale(q, a):
            which = 2 if q % 2 else a
            return scale[:, q // 2, which:which + 1]

        def unread(first, n):
            return w_lo[:, first:first + n].bitcast(mybir.dt.bfloat16)

        xT = w_hi[:, E * WE - XT * 4 * 2 * P:].bitcast(F32).rearrange("p (r c) -> p r c", r=XT)
        gates_t = w_lo[0:E, 8 * CHUNK:8 * CHUNK + 2 * N].bitcast(F32)

        def ej(ap):
            return ap.rearrange("p (e j) -> p e j", e=E)

        def je(ap):
            return ap.rearrange("p (e j) -> p j e", e=E)

        def by_half(table):
            return table[:, :].rearrange("p (t u) -> p u t", u=SUB)

        def over_j(ap):
            return ap.unsqueeze(2).to_broadcast([P, E, J])

        def over_e(ap):
            return ap.unsqueeze(1).to_broadcast([P, E, J])

        bank = [ctx.enter_context(nc.psum_tensor(f"bank{b}", [P, 512], F32)) for b in range(8)]
        ps_gate, ps_genre = bank[6][:, 0:E * J], bank[7][:, 0:E]
        ps_behind, ps_total = bank[4][:, 0:E * J], bank[4][:, E * J:2 * E * J]
        ps_slots = bank[3][:, 0:3 * COLS].rearrange("p (u c) -> p u c", u=SUB)
        ps_h = [[bank[0], bank[1]], [bank[2], bank[3]]]
        ps_x, ps_y = bank[4], bank[5]

        s_const = sem("s_const")
        s_cid = sem("s_cid")
        s_small = sem("s_small")
        s_x = [sem(f"s_x{c}") for c in range(Q4)]
        s_w = [sem(f"s_w{c}") for c in range(STAGES)]
        s_out0 = sem("s_out0")
        s_b3 = sem("s_b3")
        s_wgs = sem("s_wgs")
        s_xtp = sem("s_xtp")
        s_xts = sem("s_xts")
        s_genre = sem("s_genre")
        s_gmm = sem("s_gmm")
        s_gts = sem("s_gts")
        s_gate = sem("s_gate")
        s_ssq = sem("s_ssq")
        s_var = sem("s_var")
        s_pow = sem("s_pow")
        s_wsq = sem("s_wsq")
        s_pool = sem("s_pool")
        s_wsc = sem("s_wsc")
        s_whi = sem("s_whi")
        s_low_p = sem("s_low_p")
        s_low_v = sem("s_low_v")
        s_dve = sem("s_dve")
        s_diff = sem("s_diff")
        s_exp = sem("s_exp")
        s_sel = sem("s_sel")
        s_cnt = sem("s_cnt")
        s_hot = sem("s_hot")
        s_inv = sem("s_inv")
        s_norm = sem("s_norm")
        s_sx = sem("s_sx")
        s_from = sem("s_from")
        s_tab = sem("s_tab")
        s_own = sem("s_own")
        s_idx = sem("s_idx")
        s_prm = sem("s_prm")
        s_cw = sem("s_cw")
        s_xg = [sem(f"s_xg{s}") for s in range(RING)]
        s_xp = sem("s_xp")
        s_xhi = sem("s_xhi")
        s_xs = sem("s_xs")
        s_l1 = sem("s_l1")
        s_h1f = sem("s_h1f")
        s_h1h = sem("s_h1h")
        s_h1 = sem("s_h1")
        s_l2 = sem("s_l2")
        s_h2f = sem("s_h2f")
        s_h2h = sem("s_h2h")
        s_h2 = sem("s_h2")
        s_l3 = sem("s_l3")
        s_y32 = sem("s_y32")
        s_y = sem("s_y")
        s_add = sem("s_add")

        def by_gpsimd(q, a):
            return q < SHARED or (q < EARLY and a == 0)

        def lows(q):
            by_pool = sum(by_gpsimd(c, a) for c in range(q + 1) for a in range(2))
            return by_pool, 2 * (q + 1) - by_pool

        def wait_lows(engine, q):
            by_pool, by_dve = lows(q)
            engine.wait_ge(s_low_p, by_pool)
            if by_dve:
                engine.wait_ge(s_low_v, by_dve)

        block = ctx.enter_context(nc.Block())

        @block.sync
        def _(sp):
            for c in range(Q4):
                js = J // Q4
                if c == 1:
                    sp.dma_start(packed[:, :], small_in).then_inc(s_small, 16)
                sp.dma_start(area[:, c * js * H:(c + 1) * js * H],
                             x.rearrange("(p j) h -> p (j h)", p=P)[:, c * js * H:(c + 1) * js * H])\
                  .then_inc(s_x[c], 16)
            for q in range(CHUNKS):
                if q >= STAGES:
                    wait_lows(sp, q - STAGES)
                sp.dma_start(stage[:, q % STAGES, :], weights[q]).then_inc(s_w[q % STAGES], 16)
                if q == STAGES - 1:
                    sp.dma_start(prm[:, :, 12:PRM], b3.unsqueeze(0).to_broadcast([P, E, H])).then_inc(s_b3, 16)
                for n, after in enumerate(OUT_AT):
                    if after == q:
                        rows = slice(n * N // len(OUT_AT), (n + 1) * N // len(OUT_AT))
                        sp.dma_start(out[rows, :], x[rows, :]).then_inc(s_out0, 16)

        @block.gpsimd
        def _(pool):
            chain = [0]

            def link(ins):
                chain[0] += 1
                ins.then_inc(s_pool, 1)
                pool.wait_ge(s_pool, chain[0])

            link(pool.memset(ident[:, :], 0.0))
            pool.affine_select(out=ident[:, :], in_=ident[:, :], compare_op=ALU.not_equal, fill=1.0,
                               base=0, pattern=[[-1, P]], channel_multiplier=1).then_inc(s_cid, 1)
            link(pool.memset(halves[:, :], -0.5))
            pool.memset(ones16[:, :], 1.0).then_inc(s_const, 1)
            link(pool.memset(behind[:, :], 0.0))
            pool.affine_select(out=behind[:, :], in_=behind[:, :], compare_op=ALU.is_gt, fill=-1.0,
                               base=0, pattern=[[1, P]], channel_multiplier=-1).then_inc(s_const, 1)
            pool.iota(iota_r[:, :], pattern=[[1, T]], base=0, channel_multiplier=0,
                      allow_small_or_imprecise_dtypes=True).then_inc(s_const, 1)
            pool.iota(iota_c[:, :], pattern=[[1, TILES]], base=0, channel_multiplier=0,
                      allow_small_or_imprecise_dtypes=True).then_inc(s_const, 1)
            pool.iota(rank[:, :], pattern=[[-1, E]], base=E, channel_multiplier=0,
                      allow_small_or_imprecise_dtypes=True).then_inc(s_const, 1)

            def power_of_two(to, exponent, square):
                link(pool.tensor_scalar(exponent, square.bitcast(I32), -0.5 * 2.0 ** -MANT, 1.5 * BIAS,
                                        ALU.mult, ALU.add))
                return pool.tensor_scalar(to.bitcast(I32), exponent, float(TOP_LOG), 2.0 ** MANT, ALU.add, ALU.mult)

            def inverse(to, exponent):
                return pool.tensor_scalar(to.bitcast(I32), exponent, -2.0 ** MANT,
                                          (2.0 * BIAS - TOP_LOG) * 2.0 ** MANT, ALU.mult, ALU.add)

            def weight_scales(q):
                e, to, w = q // 2, 2 * (q % 2), 2 - q % 2
                pool.wait_ge(s_wsq, 2 * q + 2)
                link(pool.partition_all_reduce(fsq[:, q, :], wsq[:, q, :], P, RED.add))
                if q % 2:
                    link(pool.tensor_tensor(fsq[:, q, 0:1], fsq[:, q, 0:1], fsq[:, q, 1:2], ALU.add))
                power_of_two(scale[:, e, to:to + w], expo[:, e, to:to + w], fsq[:, q, 0:w]).then_inc(s_wsc, 1)

            pool.iota(tokv[:, :], pattern=[[1, J]], base=-N // 2, channel_multiplier=J,
                      allow_small_or_imprecise_dtypes=True).then_inc(s_const, 1)
            pool.iota(k_tile[:, :], pattern=[[T, MAXT]], base=0, channel_multiplier=0,
                      allow_small_or_imprecise_dtypes=True).then_inc(s_const, 1)
            pool.iota(i_tile[:, :], pattern=[[1, TILES]], base=0, channel_multiplier=0,
                      allow_small_or_imprecise_dtypes=True).then_inc(s_const, 1)

            def parameters(first, n):
                es = slice(first, first + n)
                one, two = bound[:, es, 0], bound[:, es, 1]
                w1_sq, w2_sq = fsq[:, 2 * first:2 * (first + n):2, 0], fsq[:, 2 * first + 1:2 * (first + n):2, 0]
                link(pool.tensor_scalar(one, w1_sq, xmax4, None, ALU.mult))
                link(pool.tensor_tensor(one, one, whole[:, es], ALU.add))
                link(pool.tensor_tensor(two, one, w2_sq, ALU.mult))
                link(pool.tensor_tensor(two, two, whole[:, E + first:E + first + n], ALU.add))
                link(power_of_two(scale[:, es, 3:5], expo[:, es, 3:5], bound[:, es, :]))
                link(inverse(inv_scale[:, es, :], expo[:, es, :]))
                c1, c2, c3 = (prm[:, es, c] for c in range(3))
                s1, s3, s2, sh1, sh2 = (scale[:, es, c] for c in range(5))
                inv_s1, inv_s3, inv_s2, inv_sh1, inv_sh2 = (inv_scale[:, es, c] for c in range(5))
                pool.tensor_scalar(c1, sh1, inv_sx, None, ALU.mult)
                pool.tensor_tensor(c2, sh2, inv_sh1, ALU.mult)
                pool.tensor_tensor(c3, inv_sh2, inv_s3, ALU.mult)
                for at, sh in ((4, sh1), (8, sh2)):
                    bias = prm[:, es, at:at + 4]
                    link(pool.tensor_tensor(bias, bias, sh.unsqueeze(2).to_broadcast([P, n, 4]), ALU.mult))
                pool.tensor_tensor(c1, c1, inv_s1, ALU.mult)
                return pool.tensor_tensor(c2, c2, inv_s2, ALU.mult)

            def low_parts(q):
                for a in range(2):
                    if by_gpsimd(q, a):
                        at_w = q * CHUNK + a * HALF
                        pool.wait_ge(s_whi, 2 * q + a + 1)
                        pool.tensor_tensor(w_lo[:, at_w:at_w + HALF], stage[:, q % STAGES, a * HALF:(a + 1) * HALF],
                                           w_hi[:, at_w:at_w + HALF], ALU.subtract).then_inc(s_low_p, 1)

            def inverse_rms(c):
                pool.wait_ge(s_var, c + 1)
                js = slice(c * J // 4, (c + 1) * J // 4)
                pool.tensor_tensor(rstd[:, js], var[:, js], halves[:, js], ALU.pow).then_inc(s_pow, 1)

            for c in range(3):
                inverse_rms(c)
            weight_scales(0)
            inverse_rms(3)
            weight_scales(1)
            low_parts(0)
            pool.wait_ge(s_norm, 1)
            link(pool.partition_all_reduce(xmax_all, xmax, P, RED.max))
            link(pool.partition_all_reduce(whole, part, P, RED.add))
            pool.tensor_scalar(xmax4, xmax_all, 4.0, None, ALU.mult)
            link(power_of_two(sx, xexpo, xmax_all))
            link(inverse(inv_sx, xexpo))
            pool.memset(prm[:, :, 3:4], 0.0).then_inc(s_sx, 1)
            for q in range(2, EARLY):
                weight_scales(q)
                low_parts(q - 1)
                if q == EARLY - 2:
                    parameters(0, EARLY // 2 - 1)
            low_parts(EARLY - 1)

            def copy_columns(to, table, i, signal):
                pool.tensor_copy(to, table[:, bass.ds(i * SUB, SUB)]).then_inc(signal, 1)

            def gather(i, s, copied):
                pool.wait_ge(s_idx, copied)
                pool.sem_inc(s_own, 1)
                for u in range(SUB):
                    pool.indirect_dma_start(
                        out=xg[:, s, u, :], out_offset=None, in_=x,
                        in_offset=bass.IndirectOffsetOnAxis(ap=cfrom[:, s, u:u + 1].bitcast(U32), axis=0),
                    ).then_inc(s_xg[s], 16)

            def copy_parameters(i, s):
                e = pool.value_load(etile[0:1, bass.ds(i, 1)], min_val=0, max_val=E - 1)
                pool.tensor_copy(cprm[:, s, :], prm[:, :, :].rearrange("p e c -> p (e c)")
                                 [:, bass.ds(e * PRM, PRM)]).then_inc(s_prm, 1)

            def add_rows(i, s):
                for u in range(SUB):
                    pool.indirect_dma_start(
                        out=out, out_offset=bass.IndirectOffsetOnAxis(ap=cto[:, s, u:u + 1].bitcast(U32), axis=0),
                        in_=yb[:, s, u, :], in_offset=None, bounds_check=N - 1, oob_is_err=False,
                        compute_op=ALU.add,
                    ).then_inc(s_add, 16)

            def step(i, s, first=False, late=None, next2=True, next3=True):
                s2 = (s + 2) % RING
                if late is not None:
                    weight_scales(late)
                copy_columns(cto[:, s, :], tab_to, i, s_idx)
                if next3:
                    pool.wait_ge(s_xp, i + 1)
                    copy_columns(cfrom[:, s, :], tab_from, i + 3, s_idx)
                    gather(i + 3, s, RING + 2 * i + 2)
                else:
                    last = TILES - RING
                    pool.wait_ge(s_idx, RING + 2 * last + (i - last) + 1)
                if late is not None and late % 2:
                    link(parameters(late // 2, 1))
                if next2:
                    copy_parameters(i + 2, s2)
                pool.wait_ge(s_y, 2 * i + 3)
                pool.sem_inc(s_own, 1)
                if not first:
                    pool.wait_ge(s_add, i * SUB * 16)
                    pool.sem_inc(s_own, 1)
                if next2:
                    copy_columns(cw[:, s2, :], tab_w, i + 2, s_cw)
                add_rows(i, s)

            pool.wait_ge(s_from, 1)
            for i in range(RING):
                copy_columns(cfrom[:, i, :], tab_from, i, s_idx)
                gather(i, i, i + 1)
                if i == 0:
                    weight_scales(EARLY)
            pool.wait_ge(s_tab, 1)
            pool.wait_ge(s_b3, 16)
            for i in range(2):
                copy_parameters(i, i)
                copy_columns(cw[:, i, :], tab_w, i, s_cw)
            weight_scales(EARLY + 1)
            parameters(EARLY // 2 - 1, 2)
            pool.wait_ge(s_out0, len(OUT_AT) * 16)
            for i in range(PEELED):
                step(i, i % RING, first=(i == 0), late=LATE.get(i))
            with pool.Fori(PEELED // RING, GROUPS - 1, 1) as g:
                for s in range(RING):
                    step(g * RING + s, s)
            for s in range(RING):
                i = TILES - RING + s
                step(i, s, next2=i + 2 < TILES, next3=False)
            pool.wait_ge(s_add, TILES * SUB * 16)

        @block.scalar
        def _(act):
            act.dma_start(cond_g[:, :], cond_in).then_inc(s_small, 16)

            for j in range(J):
                if j % 4 == 0:
                    act.wait_ge(s_x[j // 4], 16)
                act.activation(unread(E * WE - (J - j) * H, H), x_sb[:, j, :], ACT.Square,
                               accum_out=ssq[:, j:j + 1]).then_inc(s_ssq, 1)

            def squares(q):
                act.wait_ge(s_w[q % STAGES], 16 * (q // STAGES + 1))
                for a in range(2):
                    act.activation(unread(q * CHUNK + a * HALF, HALF),
                                   stage[:, q % STAGES, a * HALF:(a + 1) * HALF], ACT.Square,
                                   accum_out=wsq[:, q, a:a + 1]).then_inc(s_wsq, 1)

            def high_parts(q):
                act.wait_ge(s_wsc, q + 1)
                for a in range(2):
                    half = stage[:, q % STAGES, a * HALF:(a + 1) * HALF]
                    ins = act.activation(w_hi[:, q * CHUNK + a * HALF:q * CHUNK + (a + 1) * HALF], half, ACT.Copy,
                                         scale=chunk_scale(q, a))
                    if by_gpsimd(q, a):
                        ins = act.activation(half, half, ACT.Copy, scale=chunk_scale(q, a))
                    ins.then_inc(s_whi, 1)

            for q in range(EARLY):
                squares(q)
                if q >= 1:
                    high_parts(q - 1)
                if q == EXP_AFTER:
                    act.wait_ge(s_diff, 1)
                    act.activation(ex, cand_ex, ACT.Exp).then_inc(s_exp, 1)
            high_parts(EARLY - 1)
            squares(EARLY)

            def x_high(i):
                act.wait_ge(s_xp, i + 1)
                act.activation(xt_hi, ps_x[:, :], ACT.Copy, scale=sx).then_inc(s_xhi, 1)

            def activate(i, slot, layer):
                if layer == 0:
                    act.wait_ge(s_prm, i + 1)
                done, signal, to = ((s_l1, s_h1f, h1_32), (s_l2, s_h2f, h2_32))[layer]
                for b in range(2):
                    act.wait_ge(done, 2 * i + b + 1)
                    for a in range(2):
                        m = 2 * b + a
                        act.activation(to[:, m * T:(m + 1) * T], ps_h[layer][b][:, a * T:(a + 1) * T], ACT.Relu,
                                       bias=cprm[:, slot, 4 + 4 * layer + m:5 + 4 * layer + m],
                                       scale=cprm[:, slot, layer:layer + 1]).then_inc(signal, 1)

            def weigh(i, slot):
                act.wait_ge(s_y32, i + 2)
                act.wait_ge(s_cw, i + 1)
                for u in range(SUB):
                    act.activation(yb[:, slot, u, :], y32[:, u * H:(u + 1) * H], ACT.Copy,
                                   scale=cw[:, slot, u:u + 1]).then_inc(s_y, 1)

            def step(i, s, late=None, next1=True, next2=True):
                activate(i, s, 1)
                if next1:
                    activate(i + 1, (s + 1) % RING, 0)
                if next2:
                    x_high(i + 2)
                if late is not None:
                    late_chunk(late)
                weigh(i, s)

            def late_chunk(q):
                high_parts(q)
                if q + 1 < CHUNKS:
                    squares(q + 1)

            act.wait_ge(s_tab, 1)
            act.wait_ge(s_sx, 1)
            act.sem_inc(s_y, 1)
            high_parts(EARLY)
            x_high(0)
            squares(EARLY + 1)
            activate(0, 0, 0)
            x_high(1)
            late_chunk(EARLY + 1)
            for i in range(PEELED):
                step(i, i % RING, late=LATE.get(i))
            with act.Fori(PEELED // RING, GROUPS - 1, 1) as g:
                for s in range(RING):
                    step(g * RING + s, s)
            for s in range(RING):
                i = TILES - RING + s
                step(i, s, next1=i + 1 < TILES, next2=i + 2 < TILES)

        @block.vector
        def _(dve):
            chain = [0]

            def link(ins):
                chain[0] += 1
                ins.then_inc(s_dve, 1)
                dve.wait_ge(s_dve, chain[0])

            def low_parts(q):
                for a in range(2):
                    if not by_gpsimd(q, a):
                        at_w = q * CHUNK + a * HALF
                        dve.wait_ge(s_whi, 2 * q + a + 1)
                        dve.scalar_tensor_tensor(
                            w_lo[:, at_w:at_w + HALF], stage[:, q % STAGES, a * HALF:(a + 1) * HALF],
                            chunk_scale(q, a), w_hi[:, at_w:at_w + HALF], ALU.mult, ALU.subtract)\
                            .then_inc(s_low_v, 1)

            dve.memset(ones8, 1.0)
            link(dve.memset(restart[:, :], 1.0))
            link(dve.memset(ej(restart[:, :])[:, :, 0:1], 0.0))
            dve.wait_ge(s_const, 8)
            link(dve.tensor_scalar(tokv[P // 2:P, :], tokv[P // 2:P, :], 1.0, None, ALU.add))
            for k in range(2):
                dve.tensor_copy(values[:, k * J:(k + 1) * J, 0], tokv[:, :])

            def small_inputs():
                dve.wait_ge(s_small, 2 * 16)
                for k in range(KH):
                    ins = dve.tensor_scalar(wgs[:, k, :], wg_in[:, k, :], rmsw[:, k:k + 1], None, ALU.mult)
                ins.then_inc(s_wgs, 1)
                dve.tensor_copy(prm[:, :, 4:12], bias_in)
                bsq = bias_sq[:, 0:64].rearrange("p (l e c) -> p l e c", l=2, e=E)
                link(dve.tensor_tensor(bsq, bias_in.rearrange("p e (l c) -> p l e c", l=2),
                                       bias_in.rearrange("p e (l c) -> p l e c", l=2), ALU.mult))
                link(dve.tensor_reduce(part.rearrange("p (l e) -> p l e", l=2), bsq, AX.X, ALU.add))
                dve.tensor_scalar(part[:, 0:E], part[:, 0:E], 4.0, None, ALU.mult)
                link(dve.tensor_scalar(part[:, E:], part[:, E:], 2.0, None, ALU.mult))

            def variances(c):
                js = slice(c * J // 4, (c + 1) * J // 4)
                dve.wait_ge(s_ssq, (c + 1) * J // 4)
                dve.tensor_scalar(var[:, js], ssq[:, js], 1.0 / H, EPS, ALU.mult, ALU.add).then_inc(s_var, 1)

            def newton():
                dve.wait_ge(s_pow, 4)
                link(dve.tensor_tensor(rms_tmp, rstd, rstd, ALU.mult))
                link(dve.tensor_tensor(rms_tmp, rms_tmp, var, ALU.mult))
                link(dve.tensor_scalar(rms_tmp, rms_tmp, -0.5, 1.5, ALU.mult, ALU.add))
                link(dve.tensor_tensor(rstd, rstd, rms_tmp, ALU.mult))

            def gates_out(jq):
                dve.wait_ge(s_gmm, 2 * jq + 2)
                dve.tensor_copy(gates_t[:, jq * 4 * P:(jq + 1) * 4 * P], bank[4 + jq % 2][0:E, :]).then_inc(s_gts, 1)

            for jq in range(Q4):
                for k in range(KH):
                    u = KH * jq + k
                    dve.wait_ge(s_xtp, u + 1)
                    if u >= XT:
                        dve.wait_ge(s_gmm, u - XT + 1)
                    dve.tensor_copy(xT[:, u % XT, :], bank[u % 4][:, :]).then_inc(s_xts, 1)
                if jq == 0:
                    small_inputs()
                else:
                    gates_out(jq - 1)
                if jq in VARIANCES_AT:
                    variances(VARIANCES_AT.index(jq))
            dve.tensor_reduce(xmax, ssq[:, :], AX.X, ALU.max).then_inc(s_norm, 1)
            dve.wait_ge(s_genre, 1)
            link(dve.tensor_copy(genre, ps_genre))
            newton()
            gates_out(Q4 - 1)
            dve.wait_ge(s_gate, 1)
            link(dve.tensor_tensor(ej(gate), ps_gate.rearrange("p (j e) -> p e j", e=E), over_e(rstd), ALU.mult))
            link(dve.tensor_tensor(ej(gate), ej(gate), over_j(genre), ALU.add))

            def pick(scores, top, onehot, best):
                link(dve.tensor_reduce(top, je(scores), AX.X, ALU.max))
                link(dve.tensor_tensor(ej(cand), ej(scores), over_e(top), ALU.is_equal))
                link(dve.tensor_tensor(ej(cand), ej(cand), over_j(rank[:, :]), ALU.mult))
                link(dve.tensor_reduce(best, je(cand), AX.X, ALU.max))
                link(dve.tensor_tensor(ej(onehot), ej(cand), over_e(best), ALU.is_equal))

            pick(gate, m1, oh1, r1)
            link(dve.scalar_tensor_tensor(second, oh1, -3e38, gate, ALU.mult, ALU.add))
            pick(second, m2, oh2, r1)
            dve.tensor_tensor(cand_ex[:, 0:E * J].rearrange("p (e j) -> p e j", e=E), ej(gate), over_e(m1),
                              ALU.subtract)
            dve.tensor_tensor(cand_ex[:, E * J:], m2, m1, ALU.subtract).then_inc(s_diff, 1)
            dve.tensor_tensor(sel16, oh1, oh2, ALU.add).then_inc(s_sel, 1)
            dve.wait_ge(s_exp, 1)
            link(dve.tensor_reduce(rs, je(ex[:, 0:E * J]), AX.X, ALU.add))
            link(dve.reciprocal(rs, rs))
            link(dve.tensor_scalar(wt[:, 0:J], rs, WSCALE, None, ALU.mult))
            link(dve.tensor_tensor(wt[:, J:2 * J], ex[:, E * J:], wt[:, 0:J], ALU.mult))
            link(dve.tensor_copy(values[:, :, 1], wt))
            link(dve.tensor_copy(wt_h, values[:, :, 1]))
            link(dve.tensor_tensor(values[:, :, 2], wt, wt_h, ALU.subtract))
            dve.wait_ge(s_cnt, 1)
            link(dve.tensor_tensor_scan(upto, restart[:, :], ps_total, 0.0, ALU.mult, ALU.add))
            count = ej(upto)[:, :, J - 1:J]
            link(dve.tensor_tensor(cmp_n.rearrange("p (e k) -> p e k", e=E), count.to_broadcast([P, E, MAXT]),
                                   k_tile[:, :].unsqueeze(1).to_broadcast([P, E, MAXT]), ALU.is_gt))
            link(dve.tensor_reduce(ntile, cmp_n.rearrange("p (e k) -> p e k", e=E), AX.X, ALU.add))
            link(dve.tensor_scalar(ntile, ntile, 1.0, None, ALU.max))
            link(dve.tensor_tensor_scan(tend, ones8, ntile, 0.0, ALU.mult, ALU.add))
            link(dve.tensor_tensor(ntile, tend, ntile, ALU.subtract))
            link(dve.tensor_scalar(ntile, ntile, float(T), None, ALU.mult))
            link(dve.tensor_tensor(upto, upto, ps_behind, ALU.add))
            link(dve.tensor_tensor(ej(upto), ej(upto), over_j(ntile), ALU.add))
            both = area[:, 2 * E * J:4 * E * J].rearrange("p (k c) -> p k c", k=2)
            link(dve.tensor_tensor(pairs.rearrange("p (k c) -> p k c", k=2), both,
                                   upto.unsqueeze(1).to_broadcast([P, 2, E * J]), ALU.mult))
            link(dve.tensor_reduce(slot_f.rearrange("p (k j) -> p k j", k=2),
                                   pairs.rearrange("p (k e j) -> p k j e", k=2, e=E), AX.X, ALU.add))
            link(dve.tensor_copy(slot_i, slot_f))
            dve.tensor_scalar(part_i, slot_i, T - 1, None, ALU.bitwise_and)
            link(dve.tensor_scalar(slot_i, slot_i, T.bit_length() - 1, None, ALU.logical_shift_right))
            dve.tensor_copy(row_f, part_i)
            link(dve.tensor_copy(tile16, slot_i))
            for b in range(2 * J // BATCH):
                ns = slice(b * BATCH, (b + 1) * BATCH)
                if b >= 2:
                    dve.wait_ge(s_inv, b - 1)
                for n in range(BATCH):
                    at_n = b * BATCH + n
                    dve.tensor_scalar(hot_r[:, b % 2, n, :], iota_r[:, :], row_f[:, at_n:at_n + 1], None, ALU.is_equal)
                link(dve.tensor_tensor(hot_c[:, b % 2], iota_c[:, :].unsqueeze(1).to_broadcast([P, BATCH, TILES]),
                                       tile16[:, ns].unsqueeze(2).to_broadcast([P, BATCH, TILES]), ALU.is_equal))
                ins = dve.tensor_tensor(hot_q[:, b % 2],
                                        hot_c[:, b % 2].unsqueeze(2).to_broadcast([P, BATCH, 3, TILES]),
                                        values[:, ns, :].unsqueeze(3).to_broadcast([P, BATCH, 3, TILES]), ALU.mult)
                ins.then_inc(s_hot, 1)
                if b in BATCH_CHUNKS:
                    low_parts(BATCH_CHUNKS[b])
            link(dve.tensor_tensor(cmp_t.rearrange("p (i e) -> p i e", e=E),
                                   i_tile[:, :].unsqueeze(2).to_broadcast([P, TILES, E]),
                                   tend.unsqueeze(1).to_broadcast([P, TILES, E]), ALU.is_ge))
            link(dve.tensor_reduce(et_f, cmp_t.rearrange("p (i e) -> p i e", e=E), AX.X, ALU.add))
            link(dve.tensor_scalar(etile[:, :], et_f, float(E - 1), None, ALU.min))
            dve.wait_ge(s_inv, 2 * J // BATCH)
            inv = ps_slots.rearrange("p u (v t) -> p u v t", v=3)
            link(dve.tensor_scalar(pos_f, inv[:, :, 0, :], 0.0, None, ALU.is_gt))
            link(dve.scalar_tensor_tensor(code, inv[:, :, 0, :], float(N // 2), pos_f, ALU.add, ALU.subtract))
            link(dve.tensor_copy(by_half(tab_from), code))
            dve.sem_inc(s_from, 1)
            link(dve.tensor_scalar(pad, inv[:, :, 0, :], 0.0, float(FAR), ALU.is_equal, ALU.mult))
            dve.tensor_tensor(by_half(tab_to), code, pad, ALU.add)
            link(dve.tensor_copy(wsum, inv[:, :, 2, :]))
            link(dve.tensor_tensor(wsum, wsum, inv[:, :, 1, :], ALU.add))
            dve.tensor_scalar(by_half(tab_w), wsum, 1.0 / WSCALE, None, ALU.mult).then_inc(s_tab, 1)

            for q in range(EARLY):
                if q >= SHARED and q not in BATCH_CHUNKS.values():
                    low_parts(q)

            def x_low(i):
                dve.wait_ge(s_xhi, i + 1)
                dve.scalar_tensor_tensor(xt_lo, ps_x[:, :], sx, xt_hi, ALU.mult, ALU.subtract).then_inc(s_xs, 1)

            def split(i, layer):
                full, half_done, signal = ((s_h1f, s_h1h, s_h1), (s_h2f, s_h2h, s_h2))[layer]
                h, hi, lo = ((h1_32, h1_hi, h1_lo), (h2_32, h2_hi, h2_lo))[layer]
                for b in range(2):
                    cols = slice(b * 2 * T, (b + 1) * 2 * T)
                    dve.wait_ge(full, 4 * i + 2 * b + 2)
                    dve.tensor_copy(hi[:, cols], h[:, cols]).then_inc(half_done, 1)
                    dve.wait_ge(half_done, 2 * i + b + 1)
                    dve.tensor_tensor(lo[:, cols], h[:, cols], hi[:, cols], ALU.subtract).then_inc(signal, 1)

            def finish(i, slot):
                dve.wait_ge(s_l3, i + 1)
                dve.wait_ge(s_y, 2 * i + 1)
                dve.scalar_tensor_tensor(
                    y32.rearrange("p (u h) -> p u h", u=SUB), ps_y[:, :].rearrange("p (u h) -> p u h", u=SUB),
                    cprm[:, slot, 2:3], cprm[:, slot, 12:PRM].unsqueeze(1).to_broadcast([P, SUB, H]),
                    ALU.mult, ALU.add).then_inc(s_y32, 1)

            def step(i, s, late=None, next1=True, next2=True):
                split(i, 1)
                if next1:
                    split(i + 1, 0)
                if next2:
                    x_low(i + 2)
                if late is not None:
                    low_parts(late)
                finish(i, s)

            dve.wait_ge(s_sx, 1)
            dve.sem_inc(s_y32, 1)
            x_low(0)
            low_parts(EARLY)
            split(0, 0)
            x_low(1)
            low_parts(EARLY + 1)
            for i in range(PEELED):
                step(i, i % RING, late=LATE.get(i))
            with dve.Fori(PEELED // RING, GROUPS - 1, 1) as g:
                for s in range(RING):
                    step(g * RING + s, s)
            for s in range(RING):
                i = TILES - RING + s
                step(i, s, next1=i + 1 < TILES, next2=i + 2 < TILES)

        @block.tensor
        def _(pe):
            def keep_busy(n, operand):
                for _ in range(n):
                    nc.tensor.matmul(bank[7][:, 0:operand.shape[-1]], operand[:, 0:P], operand, start=True, stop=True)

            def transposes(jq):
                pe.wait_ge(s_x[jq], 16)
                for k in range(KH):
                    u = KH * jq + k
                    if u >= 4:
                        pe.wait_ge(s_xts, u - 3)
                    for d in range(4):
                        ins = nc.tensor.transpose(bank[u % 4][:, d * P:(d + 1) * P],
                                                  x_sb[:, 4 * jq + d, k * P:(k + 1) * P], ident[:, :])
                    ins.then_inc(s_xtp, 1)

            def gates(jq):
                if jq >= 2:
                    pe.wait_ge(s_gts, jq - 1)
                for k in range(KH):
                    u = KH * jq + k
                    pe.wait_ge(s_xts, u + 1)
                    nc.tensor.matmul(bank[4 + jq % 2][0:E, :], wgs[:, k, :], xT[:, u % XT, :],
                                     start=(k == 0), stop=(k == KH - 1)).then_inc(s_gmm, 1)

            def gates_back(jq):
                pe.wait_ge(s_gts, jq + 1)
                for j in range(4 * jq, 4 * jq + 4):
                    ins = nc.tensor.transpose(ps_gate[:, j * E:(j + 1) * E], gates_t[:, j * P:(j + 1) * P],
                                              ident[0:E, 0:E])
                return ins

            pe.wait_ge(s_const, 1)
            keep_busy(WARM_START, ones16[:, :])
            pe.wait_ge(s_cid, 1)
            transposes(0)
            pe.wait_ge(s_wgs, 1)
            nc.tensor.matmul(ps_genre, cond_s, ggw_s, start=True, stop=True).then_inc(s_genre, 1)
            for jq in range(1, Q4):
                transposes(jq)
                gates(jq - 1)
                if jq >= 2:
                    gates_back(jq - 2)
            gates(Q4 - 1)
            gates_back(Q4 - 2)
            gates_back(Q4 - 1).then_inc(s_gate, 1)
            pe.wait_ge(s_const, 8)
            pe.wait_ge(s_sel, 1)
            nc.tensor.matmul(ps_behind, behind[:, :], sel16, start=True, stop=True)
            nc.tensor.matmul(ps_total, ones16[:, :], sel16, start=True, stop=True).then_inc(s_cnt, 1)
            for b in range(2 * J // BATCH):
                pe.wait_ge(s_hot, b + 1)
                for n in range(BATCH):
                    for u in range(SUB):
                        ins = nc.tensor.matmul(ps_slots[:, u, :], hot_r[:, b % 2, n, u * P:(u + 1) * P],
                                               hot_q[:, b % 2, n].rearrange("p v c -> p (v c)"),
                                               start=(b == 0 and n == 0 and u == 0),
                                               stop=(b == 2 * J // BATCH - 1 and n == BATCH - 1 and u == SUB - 1))
                ins.then_inc(s_inv, 1)

            def transpose_x(i, slot, turn):
                pe.wait_ge(s_xg[slot], turn * SUB * 16)
                if not (isinstance(i, int) and i == 0):
                    pe.wait_ge(s_xs, i)
                for k in range(KH):
                    for u in range(SUB):
                        ins = nc.tensor.transpose(ps_x[:, k * T + u * P:k * T + (u + 1) * P],
                                                  xg[:, slot, u, k * P:(k + 1) * P], ident[:, :])
                ins.then_inc(s_xp, 1)

            def weights_at(i):
                return pe.value_load(etile[0:1, bass.ds(i, 1)], min_val=0, max_val=E - 1) * WE

            def layer(w, first, chunks, parts, banks, signal):
                hi, lo = parts
                for m in range(KM):
                    for k in range(chunks):
                        at_w = first + k * M + m * P
                        cols = slice(k * T, (k + 1) * T)
                        for n, (wp, xp) in enumerate(((w_hi, hi), (w_hi, lo), (w_lo, hi))):
                            ins = nc.tensor.matmul(
                                banks[m // 2][:, (m % 2) * T:(m % 2 + 1) * T], wp[:, bass.ds(w + at_w, P)],
                                xp[:, cols], start=(k == 0 and n == 0), stop=(k == chunks - 1 and n == 2))
                    if m % 2:
                        ins.then_inc(signal, 1)

            def layer1(i, w):
                if isinstance(i, int):
                    wait_lows(pe, 2 * min(i, E - 1) + 1)
                pe.wait_ge(s_xs, i + 1)
                layer(w, W1_AT, KH, (xt_hi, xt_lo), ps_h[0], s_l1)

            def layer2(i, w):
                pe.wait_ge(s_h1, 2 * i + 2)
                layer(w, W2_AT, KM, (h1_hi, h1_lo), ps_h[1], s_l2)

            def layer3(i, w):
                pe.wait_ge(s_h2, 2 * i + 2)
                pe.wait_ge(s_y32, i + 1)
                for u in range(SUB):
                    for k in range(KM):
                        cols = slice(k * T + u * P, k * T + (u + 1) * P)
                        for n, (hp, wp) in enumerate(((h2_hi, w_hi), (h2_hi, w_lo), (h2_lo, w_hi))):
                            ins = nc.tensor.matmul(
                                ps_y[:, u * H:(u + 1) * H], hp[:, cols],
                                wp[:, bass.ds(w + (W3_AT + k * H), H)],
                                start=(k == 0 and n == 0), stop=(k == KM - 1 and n == 2))
                ins.then_inc(s_l3, 1)

            def step(i, s, turn, next1=True, next2=True):
                w = weights_at(i)
                layer2(i, w)
                if next1:
                    layer1(i + 1, weights_at(i + 1))
                if next2:
                    transpose_x(i + 2, (s + 2) % RING, turn + (s + 2) // RING + 1)
                layer3(i, w)

            pe.wait_ge(s_tab, 1)
            transpose_x(0, 0, 1)
            layer1(0, weights_at(0))
            transpose_x(1, 1, 1)
            for i in range(PEELED):
                step(i, i % RING, i // RING)
            wait_lows(pe, CHUNKS - 1)
            with pe.Fori(PEELED // RING, GROUPS - 1, 1) as g:
                for s in range(RING):
                    step(g * RING + s, s, g)
            for s in range(RING):
                i = TILES - RING + s
                step(i, s, GROUPS - 1, next1=i + 1 < TILES, next2=i + 2 < TILES)


def kernel(x, cond_256, L0_cond_rms_w, L0_cond_wg_W, L0_cond_wg_b, L0_cond_gg_W, L0_cond_gg_b,
           L0_cond_W1, L0_cond_b1, L0_cond_W2, L0_cond_b2, L0_cond_W3, L0_cond_b3):
    import numpy as np
    import concourse.bacc as bacc
    from concourse.bass_utils import run_bass_kernel_spmd

    def chunked(w):
        return w.reshape(w.shape[0] // P, P, w.shape[1]).transpose(1, 0, 2).reshape(P, -1)

    x = np.asarray(x)
    w1, w2, w3 = (np.asarray(w) for w in (L0_cond_W1, L0_cond_W2, L0_cond_W3))
    chunks = []
    for e in range(E):
        chunks.append(np.concatenate([chunked(w1[e]), chunked(w3[e])], axis=1))
        chunks.append(chunked(w2[e]))
    x_rows = x.reshape(N, H)
    packed = np.concatenate([
        np.asarray(L0_cond_rms_w).reshape(KH, P).T,
        np.asarray(L0_cond_wg_W).reshape(KH, P, E).transpose(1, 0, 2).reshape(P, -1),
        np.stack([np.asarray(b).reshape(E, KM, P) for b in (L0_cond_b1, L0_cond_b2)], axis=1)
        .transpose(3, 0, 1, 2).reshape(P, -1)], axis=1)
    cond = np.concatenate([
        np.concatenate([np.repeat(np.asarray(cond_256).T, P // x.shape[0], axis=1), np.asarray(L0_cond_gg_W)], axis=1),
        np.concatenate([np.ones((2, P), x.dtype),
                        np.stack([np.asarray(L0_cond_wg_b), np.asarray(L0_cond_gg_b)])], axis=1)])
    arrays = {"x": x_rows, "small_in": packed, "cond_in": cond, "weights": np.stack(chunks),
              "b3": np.asarray(L0_cond_b3)}
    arrays = {name: np.ascontiguousarray(a) for name, a in arrays.items()}
    nc = bacc.Bacc("TRN2", target_bir_lowering=False, num_devices=1)
    args = [nc.dram_tensor(f"in_{name}", a.shape, F32, kind="ExternalInput").ap() for name, a in arrays.items()]
    out = nc.dram_tensor("out", (N, H), F32, kind="ExternalOutput").ap()
    build_moe(nc, *args, out)
    got = run_bass_kernel_spmd(nc, [{f"in_{name}": a for name, a in arrays.items()}], core_ids=[0])
    return got.results[0]["out"].reshape(x.shape)
```
